# Optimizing a Trainium2 kernel written in Bass

```python
import numpy as np
import jax
import jax.numpy as jnp

def _softmax(x, axis=-1):
    return jax.nn.softmax(x, axis=axis)

def _gelu(x):
    return jax.nn.gelu(x, approximate=True)

def _silu(x):
    return jax.nn.silu(x)

def _sigmoid(x):
    return jax.nn.sigmoid(x)

def _layernorm(x, axis=-1, eps=1e-05):
    m = jnp.mean(x, axis=axis, keepdims=True)
    v = jnp.var(x, axis=axis, keepdims=True)
    return (x - m) / jnp.sqrt(v + eps)

def _scatter_add(tgt, idx, src, axis=0):
    return tgt.at[idx].add(src)

def _segment_sum(src, seg, n):
    return jax.ops.segment_sum(src, seg, n)
kernel_name = 'mk_cond_seq_d1_seqx_r2_dfc1d5'

def setup_inputs(seed: int=0):
    np.random.seed(seed)
    _w = jnp.asarray

    def _rec_inputs():
        import jax
        import jax.numpy as jnp
        _rk = jax.random.key(seed)
        x = 7.22e-05 + 1 * jax.random.normal(jax.random.fold_in(_rk, 1), (64, 128, 1024), jnp.float32)
        _lenS = 128 - jax.random.randint(jax.random.fold_in(_rk, 7), (64,), 0, max(1, 128 // 4) + 1, jnp.int32)
        _lenS2 = 128 - jax.random.randint(jax.random.fold_in(_rk, 8), (64,), 0, max(1, 128 // 4) + 1, jnp.int32)
        cond_2048 = 0.0061147 + 1.02565 * jax.random.normal(jax.random.fold_in(_rk, 11), (64, 1024), jnp.float32)
        return (x, cond_2048)
    x, cond_2048 = _rec_inputs()

    def _L0_cond_setup():
        import jax, jax.numpy as jnp
        import numpy as np
        D_MODEL = 1024
        N_HEADS = 16
        N_KV_HEADS = 4
        HEAD_DIM = D_MODEL // N_HEADS
        N_GROUPS = N_HEADS // N_KV_HEADS
        BLOCK_SIZE = 128
        WINDOW = 128
        GLOBAL_EVERY = 64
        LATENT = 256
        ROPE_THETA = 10000.0
        LN_EPS = 1e-05

        def _rope_tables(T, dtype):
            freqs = 1.0 / ROPE_THETA ** (jnp.arange(0, HEAD_DIM, 2, dtype=jnp.float32) / HEAD_DIM)
            emb = jnp.arange(T, dtype=jnp.float32)[:, None] * freqs[None, :]
            cos = jnp.concatenate([jnp.cos(emb), jnp.cos(emb)], axis=-1).astype(dtype)
            sin = jnp.concatenate([jnp.sin(emb), jnp.sin(emb)], axis=-1).astype(dtype)
            return (cos, sin)

        def _rotate_half(x):
            h = x.shape[-1] // 2
            return jnp.concatenate([-x[..., h:], x[..., :h]], axis=-1)

        def _sparse_mask(T):
            idx = jnp.arange(T)
            blk = idx // BLOCK_SIZE
            future_block = blk[None, :] > blk[:, None]
            outside_window = jnp.abs(idx[None, :] - idx[:, None]) > WINDOW
            global_visible = jnp.broadcast_to((idx % GLOBAL_EVERY == 0)[None, :], (T, T))
            return outside_window & ~global_visible | future_block
        key = jax.random.key(seed)
        ks = jax.random.split(key, 9)
        B, T = (2, 1024)
        s = 0.02
        return {'x': jax.random.normal(ks[0], (B, T, D_MODEL), jnp.float32), 't_emb': jax.random.normal(ks[1], (B, D_MODEL), jnp.float32), 'W_ada': jax.random.normal(ks[2], (2 * D_MODEL, D_MODEL), jnp.float32) * s, 'b_ada': jnp.zeros((2 * D_MODEL,), jnp.float32), 'Wq': jax.random.normal(ks[3], (N_HEADS * HEAD_DIM, D_MODEL), jnp.float32) * s, 'Wkd': jax.random.normal(ks[4], (LATENT, D_MODEL), jnp.float32) * s, 'Wku': jax.random.normal(ks[5], (N_KV_HEADS * HEAD_DIM, LATENT), jnp.float32) * s, 'Wvu': jax.random.normal(ks[6], (N_KV_HEADS * HEAD_DIM, LATENT), jnp.float32) * s, 'Wo': jax.random.normal(ks[7], (D_MODEL, N_HEADS * HEAD_DIM), jnp.float32) * s}
    _L0_cond_all = _L0_cond_setup()
    _L0_cond_in = {k: v for k, v in _L0_cond_all.items() if k in ('W_ada', 'b_ada', 'Wq', 'Wkd', 'Wku', 'Wvu', 'Wo')}
    del _L0_cond_all
    return {'x': x, 'cond_2048': cond_2048, 'L0_cond_W_ada': _L0_cond_in['W_ada'], 'L0_cond_b_ada': _L0_cond_in['b_ada'], 'L0_cond_Wq': _L0_cond_in['Wq'], 'L0_cond_Wkd': _L0_cond_in['Wkd'], 'L0_cond_Wku': _L0_cond_in['Wku'], 'L0_cond_Wvu': _L0_cond_in['Wvu'], 'L0_cond_Wo': _L0_cond_in['Wo']}

def reference(x, cond_2048, L0_cond_W_ada, L0_cond_b_ada, L0_cond_Wq, L0_cond_Wkd, L0_cond_Wku, L0_cond_Wvu, L0_cond_Wo):
    import jax
    import jax.numpy as jnp

    def _L0_cond_ref(x, t_emb, W_ada, b_ada, Wq, Wkd, Wku, Wvu, Wo):
        import jax, jax.numpy as jnp
        import numpy as np
        D_MODEL = 1024
        N_HEADS = 16
        N_KV_HEADS = 4
        HEAD_DIM = D_MODEL // N_HEADS
        N_GROUPS = N_HEADS // N_KV_HEADS
        BLOCK_SIZE = 128
        WINDOW = 128
        GLOBAL_EVERY = 64
        LATENT = 256
        ROPE_THETA = 10000.0
        LN_EPS = 1e-05

        def _rope_tables(T, dtype):
            freqs = 1.0 / ROPE_THETA ** (jnp.arange(0, HEAD_DIM, 2, dtype=jnp.float32) / HEAD_DIM)
            emb = jnp.arange(T, dtype=jnp.float32)[:, None] * freqs[None, :]
            cos = jnp.concatenate([jnp.cos(emb), jnp.cos(emb)], axis=-1).astype(dtype)
            sin = jnp.concatenate([jnp.sin(emb), jnp.sin(emb)], axis=-1).astype(dtype)
            return (cos, sin)

        def _rotate_half(x):
            h = x.shape[-1] // 2
            return jnp.concatenate([-x[..., h:], x[..., :h]], axis=-1)

        def _sparse_mask(T):
            idx = jnp.arange(T)
            blk = idx // BLOCK_SIZE
            future_block = blk[None, :] > blk[:, None]
            outside_window = jnp.abs(idx[None, :] - idx[:, None]) > WINDOW
            global_visible = jnp.broadcast_to((idx % GLOBAL_EVERY == 0)[None, :], (T, T))
            return outside_window & ~global_visible | future_block
        B, T, C = x.shape
        proj = t_emb @ W_ada.T + b_ada
        scale, shift = (proj[:, :C], proj[:, C:])
        mu = jnp.mean(x, axis=-1, keepdims=True)
        var = jnp.mean(jnp.square(x - mu), axis=-1, keepdims=True)
        h = (x - mu) * jax.lax.rsqrt(var + LN_EPS)
        h = h * (1.0 + scale[:, None, :]) + shift[:, None, :]
        q = (h @ Wq.T).reshape(B, T, N_HEADS, HEAD_DIM).transpose(0, 2, 1, 3)
        c_kv = h @ Wkd.T
        k = (c_kv @ Wku.T).reshape(B, T, N_KV_HEADS, HEAD_DIM).transpose(0, 2, 1, 3)
        v = (c_kv @ Wvu.T).reshape(B, T, N_KV_HEADS, HEAD_DIM).transpose(0, 2, 1, 3)
        cos, sin = _rope_tables(T, x.dtype)
        cos, sin = (cos[None, None], sin[None, None])
        q = q * cos + _rotate_half(q) * sin
        k = k * cos + _rotate_half(k) * sin
        k_exp = jnp.repeat(k, N_GROUPS, axis=1)
        v_exp = jnp.repeat(v, N_GROUPS, axis=1)
        mask = _sparse_mask(T)
        scores = jnp.einsum('bhtd,bhsd->bhts', q, k_exp) / jnp.sqrt(jnp.asarray(HEAD_DIM, x.dtype))
        scores = jnp.where(mask[None, None], jnp.asarray(-jnp.inf, x.dtype), scores)
        attn = jax.nn.softmax(scores, axis=-1)
        y = jnp.einsum('bhts,bhsd->bhtd', attn, v_exp)
        out = y.transpose(0, 2, 1, 3).reshape(B, T, C) @ Wo.T
        return x + out
    x = _L0_cond_ref(x, cond_2048, L0_cond_W_ada, L0_cond_b_ada, L0_cond_Wq, L0_cond_Wkd, L0_cond_Wku, L0_cond_Wvu, L0_cond_Wo)
    return x

_drawn_inputs = setup_inputs


def setup_inputs(seed=0):
    import zlib

    import numpy as np

    out = dict(_drawn_inputs(seed))
    spreads = {'L0_cond_b_ada': (0.0, 0.631)}
    factors = {'L0_cond_Wq': 8.0, 'L0_cond_Wku': 8.0}
    for name, (base, spread) in spreads.items():
        noise = np.random.default_rng([zlib.crc32(name.encode()), seed]).standard_normal(out[name].shape)
        drawn = base * np.exp(spread * noise) if base else spread * noise
        out[name] = jnp.asarray(drawn.astype(out[name].dtype))
    for name, factor in factors.items():
        out[name] = (out[name] * factor).astype(out[name].dtype)
    return out
```

```python
from contextlib import ExitStack

import concourse.bass as bass
from concourse import mybir

ALU = mybir.AluOpType
ACT = mybir.ActivationFunctionType
AX = mybir.AxisListType
F32 = mybir.dt.float32
F32R = mybir.dt.float32r

P = 128
HEAD = 64
HALF = HEAD // 2
KV = 4
PER_KV = 4
LATENT = 256
LN_EPS = 1e-5
RING = 6

PASSES = ((0, 0), (0, 1), (1, 0))


def adaln_gqa_attention(nc: bass.Bass, x, cond_t, w_ada, b_ada, w_q, w_kd, w_kv, w_o, rope, out):
    B, T, C = x.shape
    KC = C // P
    KL = LATENT // P
    N2 = C // 2
    ADA = 2 * KC
    assert T == P and N2 == 512 and KV * PER_KV * HEAD == C

    ctx = ExitStack()
    with ctx:
        def sb(name, shape, dt=F32):
            return ctx.enter_context(nc.sbuf_tensor(name, shape, dt))

        def bank(name):
            return ctx.enter_context(nc.psum_tensor(name, [P, 512], F32))

        def sem(name):
            return ctx.enter_context(nc.semaphore(name))

        wq = sb("wq", [P, 2, KC, C], F32R)
        wo = sb("wo", [P, 2, KC, C], F32R)
        wkd = sb("wkd", [P, 2, KC, LATENT], F32R)
        wkv = sb("wkv", [P, KL, 2 * LATENT])
        ident = sb("ident", [P, P])
        tables = sb("tables", [P, 4, HEAD])
        scale1 = sb("scale1", [P, KC, B])
        shift = sb("shift", [P, KC, B])
        bias = sb("bias", [P, ADA])
        minus_half = sb("minus_half", [P, 1])

        xs = sb("xs", [P, C])
        stats = sb("stats", [P, 2, 6])
        mean_var = sb("mean_var", [P, 2])
        var_eps = sb("var_eps", [P, 1])
        rstd = sb("rstd", [P, 1])
        ht = sb("ht", [P, 2, KC, P], F32R)
        q_nat = sb("q_nat", [P, C])
        h_st = q_nat[:, :].rearrange("p (k t) -> p k t", t=P)
        q_rot = sb("q_rot", [P, N2])
        qt = sb("qt", [P, KC, P])
        ckv = sb("ckv", [P, LATENT])
        ckvt = sb("ckvt", [P, KL, P])
        k_nat = sb("k_nat", [P, LATENT])
        k_rot = sb("k_rot", [P, LATENT])
        kt = sb("kt", [P, 2, P])
        v = sb("v", [P, LATENT])
        neg_max = sb("neg_max", [P, KV * PER_KV])
        sums = sb("sums", [P, KV * PER_KV])
        inv_sums = sb("inv_sums", [P, KV * PER_KV])

        ring_ctx = ExitStack()
        ring = ring_ctx.enter_context(nc.sbuf_tensor("ring", [P, RING, C], F32))
        ring_ctx.close()
        probs = sb("probs", [P, KV, PER_KV, P])
        pt = sb("pt", [P, 2, PER_KV * P])
        yt = sb("yt", [P, 2, 2, PER_KV, P], F32R)
        res = sb("res", [P, C])

        A, Bk, Cb, D, E, F, G, H = (bank(f"bank_{n}") for n in "abcdefgh")
        Q_BANK = (A, Bk)
        S_BANK = (E, F)
        Y_BANK = (G, H)
        cond = qt[:, :, 0:B]

        const_loaded = sem("const_loaded")
        kvw_loaded = sem("kvw_loaded")
        chunk_loaded = [sem(f"chunk_loaded{n}") for n in range(RING)]
        x_loaded = sem("x_loaded")
        res_loaded = sem("res_loaded")
        out_stored = sem("out_stored")
        ident_zero = sem("ident_zero")
        ident_ready = sem("ident_ready")
        ada_done = sem("ada_done")
        ada_read = sem("ada_read")
        hi_split = sem("hi_split")
        lo_split = sem("lo_split")
        xt_done = sem("xt_done")
        ckv_done = sem("ckv_done")
        ckvt_done = sem("ckvt_done")
        q_done = sem("q_done")
        kv_done = sem("kv_done")
        kt_done = sem("kt_done")
        qt_done = sem("qt_done")
        s_done = sem("s_done")
        pt_done = sem("pt_done")
        pv_done = sem("pv_done")
        out_done = sem("out_done")
        half_stats = sem("half_stats")
        mean_done = sem("mean_done")
        rstd_ready = sem("rstd_ready")
        var_ready = sem("var_ready")
        half_set = sem("half_set")
        xn_ready = sem("xn_ready")
        h_lower = sem("h_lower")
        h_upper = sem("h_upper")
        h_hi = sem("h_hi")
        ht_ready = sem("ht_ready")
        ckv_ready = sem("ckv_ready")
        ckvt_ready = sem("ckvt_ready")
        q_times_table = sem("q_times_table")
        q_ready = sem("q_ready")
        k_times_table = sem("k_times_table")
        k_ready = sem("k_ready")
        kt_ready = sem("kt_ready")
        qt_ready = sem("qt_ready")
        v_ready = sem("v_ready")
        max_ready = sem("max_ready")
        exp_done = sem("exp_done")
        inv_ready = sem("inv_ready")
        probs_ready = sem("probs_ready")
        pt_ready = sem("pt_ready")
        y_hi = sem("y_hi")
        y_ready = sem("y_ready")
        out_added = sem("out_added")

        N_KD, N_Q, N_O = KC * LATENT // C, KC, KC
        KD0, Q0, O0 = ADA, ADA + N_KD, ADA + N_KD + N_Q
        CHUNKS = O0 + N_O

        def split_of(n):
            if n < Q0:
                per = C // LATENT
                k = (n - KD0) * per
                return lambda part: wkd[:, part, k:k + per, :].rearrange("p k n -> p (k n)")
            if n < O0:
                return lambda part: wq[:, part, n - Q0, :]
            return lambda part: wo[:, part, n - O0, :]

        def again(b):
            return not (isinstance(b, int) and b == 0)

        block = ctx.enter_context(nc.Block())

        @block.sync
        def _(sp):
            def load_x(b):
                if again(b):
                    sp.wait_ge(xt_done, 2 * b)
                sp.dma_start(xs[:, :], x[bass.ds(b, 1), :, :].rearrange("a t c -> (a t) c")
                             ).then_inc(x_loaded, 16)

            def load_chunk(n):
                slot, turn = n % RING, n // RING
                if turn:
                    old = n - RING
                    if old < ADA:
                        sp.wait_ge(ada_done, old + 1)
                    else:
                        sp.wait_ge(lo_split, old - ADA + 1)
                sp.dma_start(ring[:, slot, :], chunk_src(n)).then_inc(chunk_loaded[slot], 16)

            def chunk_src(n):
                if n < KD0:
                    return w_ada[n, :, :]
                if n < Q0:
                    return w_kd[n - KD0, :, :]
                if n < O0:
                    return w_q[n - Q0, :, :]
                return w_o[n - O0, :, :]

            load_x(0)
            sp.dma_start(cond, cond_t).then_inc(const_loaded, 16)
            sp.dma_start(bias[:, :], b_ada).then_inc(const_loaded, 16)
            sp.dma_start(tables[:, :, :], rope).then_inc(const_loaded, 16)
            for n in range(KD0):
                load_chunk(n)
            load_x(1)
            for n in range(KD0, O0):
                load_chunk(n)
            sp.dma_start(wkv[:, :, :], w_kv).then_inc(kvw_loaded, 16)
            for n in range(O0, CHUNKS):
                load_chunk(n)
            load_x(2)

            def slot(i, nxt, nxt2, third=True):
                if again(i):
                    sp.wait_ge(out_stored, 32 * i)
                else:
                    sp.wait_ge(lo_split, CHUNKS - ADA)
                    sp.wait_ge(hi_split, CHUNKS - ADA)
                sp.dma_start(res[:, :], x[bass.ds(i, 1), :, :].rearrange("a t c -> (a t) c")
                             ).then_inc(res_loaded, 16)
                if nxt2 and third:
                    load_x(i + 3)
                for n in range(2):
                    sp.wait_ge(out_added, 2 * i + n + 1)
                    sp.dma_start(out[bass.ds(i, 1), :, n * N2:(n + 1) * N2].rearrange("a t c -> (a t) c"),
                                 res[:, n * N2:(n + 1) * N2]).then_inc(out_stored, 16)

            slot(0, True, True)
            with sp.Fori(1, B - 3) as i:
                slot(i, True, True)
            slot(B - 3, True, True, third=False)
            slot(B - 2, True, False)
            slot(B - 1, False, False)
            sp.wait_ge(out_stored, 32 * B)

        @block.tensor
        def _(pe):
            def x_transposes(b):
                pe.wait_ge(xn_ready, b + 1)
                for half in range(2):
                    if again(b):
                        if half == 0:
                            pe.wait_ge(h_lower, b)
                        else:
                            pe.wait_ge(h_upper, b)
                    for k in range(4):
                        c = 4 * half + k
                        mm = pe.transpose(S_BANK[half][:, k * P:(k + 1) * P], xs[:, c * P:(c + 1) * P],
                                          ident[:, :])
                    mm.then_inc(xt_done, 1)

            def adaln(m):
                pe.wait_ge(chunk_loaded[m % RING], 16 * (m // RING + 1))
                if m >= 2:
                    pe.wait_ge(ada_read, m - 1)
                for k in range(KC):
                    mm = pe.matmul(Y_BANK[m % 2][:, 0:B], ring[:, m % RING, k * P:(k + 1) * P],
                                   cond[:, k, :], start=(k == 0), stop=(k == KC - 1))
                mm.then_inc(ada_done, 1)

            def split_product(bank_ap, stationary, moving, ks, n_k):
                for k in ks:
                    for s, m in PASSES:
                        mm = pe.matmul(bank_ap, stationary(s, k), moving(m, k),
                                       start=(k == 0 and (s, m) == PASSES[0]),
                                       stop=(k == n_k - 1 and (s, m) == PASSES[-1]))
                return mm

            def ckv_product(b):
                pe.wait_ge(ht_ready, 2 * b + 2)
                if again(b):
                    pe.wait_ge(v_ready, b)
                split_product(Cb[:, 0:LATENT], lambda s, k: ht[:, s, k, :],
                              lambda m, k: wkd[:, m, k, :], range(KC), KC).then_inc(ckv_done, 1)

            def q_product(b, n, ks):
                if again(b) and 0 in ks:
                    pe.wait_ge(qt_ready, 2 * (b - 1) + n + 1)
                mm = split_product(Q_BANK[n][:, :], lambda s, k: ht[:, s, k, :],
                                   lambda m, k: wq[:, m, k, n * N2:(n + 1) * N2], ks, KC)
                if KC - 1 in ks:
                    mm.then_inc(q_done, 1)

            def ckv_transposes(b):
                pe.wait_ge(ckv_ready, b + 1)
                if again(b):
                    pe.wait_ge(kt_ready, b)
                for k in range(KL):
                    mm = pe.transpose(D[:, k * P:(k + 1) * P], ckv[:, k * P:(k + 1) * P], ident[:, :])
                mm.then_inc(ckvt_done, 1)

            def kv_product(b):
                pe.wait_ge(ckvt_ready, b + 1)
                for k in range(KL):
                    mm = pe.matmul(Cb[:, :], ckvt[:, k, :], wkv[:, k, :], start=(k == 0), stop=(k == KL - 1))
                mm.then_inc(kv_done, 1)

            def k_transposes(b):
                pe.wait_ge(k_ready, b + 1)
                for p in range(2):
                    mm = pe.transpose(D[:, p * P:(p + 1) * P], k_nat[:, p * P:(p + 1) * P], ident[:, :])
                mm.then_inc(kt_done, 1)

            def q_transposes(b, n):
                pe.wait_ge(q_ready, 2 * b + n + 1)
                for j in range(4):
                    c = 4 * n + j
                    mm = pe.transpose(Q_BANK[n][:, j * P:(j + 1) * P], q_nat[:, c * P:(c + 1) * P],
                                      ident[:, :])
                mm.then_inc(qt_done, 1)

            def scores(b, p, after_exp):
                pe.wait_ge(qt_ready, 2 * b + p + 1)
                if p == 0:
                    pe.wait_ge(kt_ready, b + 1)
                    pe.wait_ge(h_lower, after_exp)
                    pe.wait_ge(h_upper, after_exp)
                else:
                    pe.wait_ge(exp_done, 4 * b + 2)
                for j in range(PER_KV):
                    for side in range(2):
                        rows = slice(side * HEAD, (side + 1) * HEAD)
                        mm = pe.matmul(S_BANK[side][:, j * P:(j + 1) * P], qt[rows, 4 * p + j, :],
                                       kt[rows, p, :], start=True, stop=True)
                        if j == PER_KV - 1:
                            mm.then_inc(s_done, 1)

            def p_transposes(b, g):
                pe.wait_ge(probs_ready, 4 * b + g + 1)
                if g < 2:
                    pe.wait_ge(exp_done, 4 * b + 4)
                else:
                    pe.wait_ge(pt_ready, 4 * b + g - 1)
                for j in range(PER_KV):
                    mm = pe.transpose(S_BANK[g % 2][:, j * P:(j + 1) * P], probs[:, g, j, :], ident[:, :])
                mm.then_inc(pt_done, 1)

            def pv_product(b, g):
                pe.wait_ge(pt_ready, 4 * b + g + 1)
                if g == 0:
                    pe.wait_ge(v_ready, b + 1)
                if again(b) and g % 2 == 0:
                    pe.wait_ge(out_added, 2 * b - 1 + g // 2)
                elif g == 0:
                    pe.wait_ge(ada_read, ADA)
                rows = slice(g % 2 * HEAD, (g % 2 + 1) * HEAD)
                pe.matmul(Y_BANK[g // 2][rows, :], v[:, g * HEAD:(g + 1) * HEAD], pt[:, g % 2, :],
                          start=True, stop=True).then_inc(pv_done, 1)

            def out_product(b, n):
                for p in range(2):
                    if n == 0:
                        pe.wait_ge(y_ready, 2 * b + p + 1)
                    mm = split_product(Y_BANK[n][:, :], lambda s, c: yt[:, s, c // 4, c % 4, :],
                                       lambda m, c: wo[:, m, c, n * N2:(n + 1) * N2],
                                       range(4 * p, 4 * p + 4), KC)
                mm.then_inc(out_done, 1)

            def project(b):
                ckv_product(b)
                q_product(b, 0, range(0, 4))
                ckv_transposes(b)
                q_product(b, 0, range(4, 8))
                kv_product(b)

            pe.wait_ge(ident_ready, 1)
            x_transposes(0)
            pe.wait_ge(const_loaded, 48)
            for m in range(ADA):
                adaln(m)
            pe.wait_ge(hi_split, N_KD)
            pe.wait_ge(lo_split, N_KD)
            ckv_product(0)
            for k in range(KC):
                pe.wait_ge(hi_split, N_KD + k + 1)
                pe.wait_ge(lo_split, N_KD + k + 1)
                q_product(0, 0, [k])
            ckv_transposes(0)
            q_product(0, 1, range(KC))
            pe.wait_ge(kvw_loaded, 16)
            kv_product(0)
            k_transposes(0)
            q_transposes(0, 0)
            q_transposes(0, 1)
            x_transposes(1)
            scores(0, 0, 2)
            pe.wait_ge(hi_split, CHUNKS - ADA)
            pe.wait_ge(lo_split, CHUNKS - ADA)

            def slot(i, nxt, nxt2):
                if nxt:
                    project(i + 1)
                scores(i, 1, None)
                if nxt:
                    q_product(i + 1, 1, range(KC))
                    k_transposes(i + 1)
                p_transposes(i, 0)
                p_transposes(i, 1)
                if nxt:
                    q_transposes(i + 1, 0)
                pv_product(i, 0)
                pv_product(i, 1)
                p_transposes(i, 2)
                p_transposes(i, 3)
                if nxt:
                    q_transposes(i + 1, 1)
                pv_product(i, 2)
                pv_product(i, 3)
                if nxt2:
                    x_transposes(i + 2)
                out_product(i, 0)
                out_product(i, 1)
                if nxt:
                    scores(i + 1, 0, i + 3 if nxt2 else B)

            slot(0, True, True)
            with pe.Fori(1, B - 2) as i:
                slot(i, True, True)
            slot(B - 2, True, False)
            slot(B - 1, False, False)

        @block.scalar
        def _(act):
            def split_hi(n):
                act.wait_ge(chunk_loaded[n % RING], 16 * (n // RING + 1))
                act.activation(split_of(n)(0), ring[:, n % RING, :], ACT.Copy).then_inc(hi_split, 1)

            def exps(b, g):
                act.wait_ge(max_ready, 4 * b + g + 1)
                if again(b):
                    act.wait_ge(pt_done, 4 * (b - 1) + g + 1)
                    act.wait_ge(inv_ready, 2 * (b - 1) + g // 2 + 1)
                for j in range(PER_KV):
                    n = PER_KV * g + j
                    ex = act.activation(probs[:, g, j, :], S_BANK[g % 2][:, j * P:(j + 1) * P], ACT.Exp,
                                        bias=neg_max[:, n:n + 1], accum_out=sums[:, n:n + 1])
                ex.then_inc(exp_done, 1)

            def copy_kt(b):
                act.wait_ge(kt_done, b + 1)
                act.activation(kt[:, :, :], D[:, 0:2 * P], ACT.Copy).then_inc(kt_ready, 1)

            def copy_qt(b, n):
                act.wait_ge(qt_done, 2 * b + n + 1)
                act.activation(qt[:, 4 * n:4 * n + 4, :], Q_BANK[n][:, :], ACT.Copy).then_inc(qt_ready, 1)

            def copy_v(b):
                act.wait_ge(k_times_table, b + 1)
                if again(b):
                    act.wait_ge(pv_done, 4 * b)
                act.activation(v[:, :], Cb[:, LATENT:2 * LATENT], ACT.Copy).then_inc(v_ready, 1)

            def copy_pt(b, g):
                act.wait_ge(pt_done, 4 * b + g + 1)
                if again(b) or g >= 2:
                    act.wait_ge(pv_done, 4 * b + g - 1)
                act.activation(pt[:, g % 2, :], S_BANK[g % 2][:, :], ACT.Copy).then_inc(pt_ready, 1)

            def split_y_hi(b, p):
                act.wait_ge(pv_done, 4 * b + 2 * p + 2)
                if again(b):
                    act.wait_ge(out_done, 2 * b)
                act.activation(yt[:, 0, p, :, :], Y_BANK[p][:, :], ACT.Copy).then_inc(y_hi, 1)

            def modulate_lower(b):
                act.wait_ge(xt_done, 2 * b + 1)
                for k in range(4):
                    h = act.activation(h_st[:, k, :], E[:, k * P:(k + 1) * P], ACT.Identity,
                                       scale=scale1[:, k, bass.ds(b, 1)], bias=shift[:, k, bass.ds(b, 1)])
                h.then_inc(h_lower, 1)

            act.wait_ge(ada_read, ADA)
            modulate_lower(0)
            for n in range(KD0, O0):
                split_hi(n)
            copy_kt(0)
            copy_qt(0, 0)
            copy_qt(0, 1)
            copy_v(0)
            act.wait_ge(ht_ready, 2)
            modulate_lower(1)
            for n in range(O0, CHUNKS):
                split_hi(n)
            act.wait_ge(lo_split, CHUNKS - ADA)

            def slot(i, nxt, nxt2):
                for g in range(KV):
                    exps(i, g)
                if nxt:
                    copy_kt(i + 1)
                copy_pt(i, 0)
                copy_pt(i, 1)
                if nxt:
                    copy_qt(i + 1, 0)
                copy_pt(i, 2)
                copy_pt(i, 3)
                split_y_hi(i, 0)
                if nxt:
                    copy_qt(i + 1, 1)
                split_y_hi(i, 1)
                if nxt:
                    copy_v(i + 1)
                if nxt2:
                    modulate_lower(i + 2)

            slot(0, True, True)
            with act.Fori(1, B - 2) as i:
                slot(i, True, True)
            slot(B - 2, True, False)
            slot(B - 1, False, False)

        @block.vector
        def _(dve):
            def row_stats(b):
                dve.wait_ge(x_loaded, 16 * (b + 1))
                for n in range(2):
                    dve.bn_stats(stats[:, n, :], xs[:, n * N2:(n + 1) * N2]).then_inc(half_stats, 1)

            def mean_and_variance(b):
                dve.bn_aggr(mean_var[:, :], stats[:, :, :].rearrange("p a s -> p (a s)")
                            ).then_inc(mean_done, 1)
                dve.wait_ge(mean_done, b + 1)
                dve.tensor_scalar(var_eps[:, :], mean_var[:, 1:2], LN_EPS, None, ALU.add
                                  ).then_inc(var_ready, 1)

            def normalise(b):
                dve.wait_ge(rstd_ready, b + 1)
                dve.tensor_scalar(xs[:, :], xs[:, :], mean_var[:, 0:1], rstd[:, 0:1],
                                  ALU.subtract, ALU.mult).then_inc(xn_ready, 1)

            def adaln_bias(m):
                dve.wait_ge(ada_done, m + 1)
                if m < KC:
                    dve.tensor_scalar(scale1[:, m, :], Y_BANK[m % 2][:, 0:B], bias[:, m:m + 1], 1.0,
                                      ALU.add, ALU.add).then_inc(ada_read, 1)
                else:
                    dve.tensor_scalar(shift[:, m - KC, :], Y_BANK[m % 2][:, 0:B], bias[:, m:m + 1], None,
                                      ALU.add).then_inc(ada_read, 1)

            def split_lo(n):
                dve.wait_ge(hi_split, n - ADA + 1)
                dve.tensor_tensor(split_of(n)(1), ring[:, n % RING, :], split_of(n)(0).bitcast(F32),
                                  ALU.subtract).then_inc(lo_split, 1)

            def modulate_upper(b):
                dve.wait_ge(xt_done, 2 * b + 2)
                for k in range(4, 8):
                    h = dve.tensor_scalar(h_st[:, k, :], F[:, (k - 4) * P:(k - 3) * P],
                                          scale1[:, k, bass.ds(b, 1)], shift[:, k, bass.ds(b, 1)],
                                          ALU.mult, ALU.add)
                h.then_inc(h_upper, 1)

            def split_h(b):
                if again(b):
                    dve.wait_ge(q_done, 2 * b)
                for half in range(2):
                    if half == 0:
                        dve.wait_ge(h_lower, b + 1)
                    else:
                        dve.wait_ge(h_upper, b + 1)
                    ks = slice(4 * half, 4 * half + 4)
                    dve.tensor_copy(ht[:, 0, ks, :], h_st[:, ks, :]).then_inc(h_hi, 1)
                for half in range(2):
                    ks = slice(4 * half, 4 * half + 4)
                    dve.wait_ge(h_hi, 2 * b + half + 1)
                    dve.tensor_tensor(ht[:, 1, ks, :], h_st[:, ks, :], ht[:, 0, ks, :].bitcast(F32),
                                      ALU.subtract).then_inc(ht_ready, 1)

            def copy_ckv(b):
                dve.wait_ge(ckv_done, b + 1)
                dve.tensor_copy(ckv[:, :], Cb[:, 0:LATENT]).then_inc(ckv_ready, 1)

            def copy_ckvt(b):
                dve.wait_ge(ckvt_done, b + 1)
                dve.tensor_copy(ckvt[:, :, :], D[:, 0:LATENT].rearrange("p (k t) -> p k t", t=P)
                                ).then_inc(ckvt_ready, 1)

            def heads(ap):
                return ap.rearrange("p (h d) -> p h d", d=HEAD)

            def turn(src, straight, turned, table, signal):
                n = heads(src).shape[1]
                dve.tensor_tensor(heads(straight), heads(src),
                                  tables[:, table:table + 1, :].broadcast_to([P, n, HEAD]), ALU.mult)
                for a in range(2):
                    mine, other = slice(a * HALF, (a + 1) * HALF), slice((1 - a) * HALF, (2 - a) * HALF)
                    last = dve.tensor_tensor(heads(turned)[:, :, mine], heads(src)[:, :, other],
                                             tables[:, table + 1:table + 2, mine].broadcast_to([P, n, HALF]),
                                             ALU.mult)
                last.then_inc(signal, 1)

            def turn_q(b, n):
                dve.wait_ge(q_done, 2 * b + n + 1)
                if again(b) or n:
                    dve.wait_ge(q_ready, 2 * b + n)
                turn(Q_BANK[n][:, :], q_nat[:, n * N2:(n + 1) * N2], q_rot[:, :], 0, q_times_table)

            def turn_k(b):
                dve.wait_ge(kv_done, b + 1)
                if again(b):
                    dve.wait_ge(kt_done, b)
                turn(Cb[:, 0:LATENT], k_nat[:, :], k_rot[:, :], 2, k_times_table)

            def maxima(b, g):
                dve.wait_ge(s_done, 4 * b + g + 1)
                if again(b):
                    dve.wait_ge(exp_done, 4 * (b - 1) + g + 1)
                dve.tensor_reduce(neg_max[:, PER_KV * g:PER_KV * (g + 1)],
                                  S_BANK[g % 2][:, :].rearrange("p (j s) -> p j s", s=P),
                                  AX.X, ALU.max, negate=True).then_inc(max_ready, 1)

            def invert(b, p):
                dve.wait_ge(exp_done, 4 * b + 2 * p + 2)
                if again(b):
                    dve.wait_ge(probs_ready, 4 * (b - 1) + 2 * p + 2)
                cols = slice(2 * p * PER_KV, 2 * (p + 1) * PER_KV)
                dve.reciprocal(inv_sums[:, cols], sums[:, cols]).then_inc(inv_ready, 1)

            def split_y_lo(b, p):
                dve.wait_ge(y_hi, 2 * b + p + 1)
                dve.tensor_tensor(yt[:, 1, p, :, :], Y_BANK[p][:, :].rearrange("p (j t) -> p j t", t=P),
                                  yt[:, 0, p, :, :].bitcast(F32), ALU.subtract).then_inc(y_ready, 1)

            def add_residual(b, n):
                dve.wait_ge(out_done, 2 * b + n + 1)
                if n == 0:
                    dve.wait_ge(res_loaded, 16 * (b + 1))
                cols = slice(n * N2, (n + 1) * N2)
                dve.tensor_tensor(res[:, cols], Y_BANK[n][:, :], res[:, cols], ALU.add
                                  ).then_inc(out_added, 1)

            row_stats(0)
            dve.wait_ge(half_stats, 2)
            mean_and_variance(0)
            normalise(0)
            dve.wait_ge(const_loaded, 48)
            for m in range(ADA):
                adaln_bias(m)
            dve.wait_ge(ada_read, ADA)
            modulate_upper(0)
            split_h(0)
            for n in range(KD0, Q0):
                split_lo(n)
            row_stats(1)
            dve.wait_ge(half_stats, 4)
            mean_and_variance(1)
            for n in range(Q0, O0):
                split_lo(n)
            normalise(1)
            copy_ckv(0)
            copy_ckvt(0)
            turn_q(0, 0)
            turn_k(0)
            turn_q(0, 1)
            dve.wait_ge(qt_done, 2)
            modulate_upper(1)
            split_h(1)
            for n in range(O0, CHUNKS):
                split_lo(n)

            def slot(i, nxt, nxt2):
                maxima(i, 0)
                maxima(i, 1)
                if nxt2:
                    row_stats(i + 2)
                    dve.wait_ge(half_stats, 2 * i + 6)
                if nxt:
                    copy_ckv(i + 1)
                if nxt2:
                    mean_and_variance(i + 2)
                if nxt:
                    copy_ckvt(i + 1)
                invert(i, 0)
                if nxt2:
                    normalise(i + 2)
                if nxt:
                    turn_q(i + 1, 0)
                    turn_k(i + 1)
                maxima(i, 2)
                maxima(i, 3)
                invert(i, 1)
                if nxt:
                    turn_q(i + 1, 1)
                split_y_lo(i, 0)
                split_y_lo(i, 1)
                if nxt2:
                    modulate_upper(i + 2)
                    split_h(i + 2)
                add_residual(i, 0)
                add_residual(i, 1)

            slot(0, True, True)
            with dve.Fori(1, B - 2) as i:
                slot(i, True, True)
            slot(B - 2, True, False)
            slot(B - 1, False, False)

        @block.gpsimd
        def _(pool):
            def inverse_deviation(b):
                pool.wait_ge(var_ready, b + 1)
                pool.tensor_tensor(rstd[:, :], var_eps[:, :], minus_half[:, :], ALU.pow
                                   ).then_inc(rstd_ready, 1)

            def normalise_probs(b, g):
                if g % 2 == 0:
                    pool.wait_ge(inv_ready, 2 * b + g // 2 + 1)
                pool.tensor_tensor(probs[:, g, :, :], probs[:, g, :, :],
                                   inv_sums[:, PER_KV * g:PER_KV * (g + 1)].rearrange("p (j o) -> p j o", o=1)
                                   .broadcast_to([P, PER_KV, P]), ALU.mult).then_inc(probs_ready, 1)

            def add_q(b, n):
                pool.wait_ge(q_times_table, 2 * b + n + 1)
                cols = slice(n * N2, (n + 1) * N2)
                pool.tensor_tensor(q_nat[:, cols], q_nat[:, cols], q_rot[:, :], ALU.add
                                   ).then_inc(q_ready, 1)

            def add_k(b):
                pool.wait_ge(k_times_table, b + 1)
                pool.tensor_tensor(k_nat[:, :], k_nat[:, :], k_rot[:, :], ALU.add).then_inc(k_ready, 1)

            pool.memset(ident[:, :], 0.0).then_inc(ident_zero, 1)
            pool.wait_ge(ident_zero, 1)
            pool.affine_select(out=ident[:, :], in_=ident[:, :], compare_op=ALU.not_equal, fill=1.0,
                               base=0, pattern=[[-1, P]], channel_multiplier=1).then_inc(ident_ready, 1)
            pool.memset(minus_half[:, :], -0.5).then_inc(half_set, 1)
            pool.wait_ge(half_set, 1)
            inverse_deviation(0)
            inverse_deviation(1)
            add_q(0, 0)
            add_k(0)
            add_q(0, 1)

            def slot(i, nxt, nxt2):
                if nxt2:
                    inverse_deviation(i + 2)
                normalise_probs(i, 0)
                normalise_probs(i, 1)
                if nxt:
                    add_q(i + 1, 0)
                    add_k(i + 1)
                normalise_probs(i, 2)
                normalise_probs(i, 3)
                if nxt:
                    add_q(i + 1, 1)

            slot(0, True, True)
            with pool.Fori(1, B - 2) as i:
                slot(i, True, True)
            slot(B - 2, True, False)
            slot(B - 1, False, False)


def rope_tables(tokens):
    import numpy as np

    freqs = (np.float32(1.0) / np.float32(10000.0) ** (np.arange(0, HEAD, 2, dtype=np.float32)
                                                       / np.float32(HEAD))).astype(np.float32)
    emb = np.arange(tokens, dtype=np.float32)[:, None] * freqs[None, :]
    cos, sin = np.cos(emb), np.sin(emb)
    cos = np.concatenate([cos, cos], axis=-1)
    sin = np.concatenate([-sin, sin], axis=-1)
    return np.ascontiguousarray(np.stack([cos, sin, cos / 8, sin / 8], axis=1), dtype=np.float32)


def kernel(**inputs):
    import numpy as np
    import concourse.bacc as bacc
    from concourse.bass_utils import run_bass_kernel_spmd

    x = np.ascontiguousarray(inputs["x"])
    rows, tokens, width = x.shape
    tiles = width // P

    def by_pairs(w):
        return w.reshape(KV // 2, 2, PER_KV, HEAD, -1).transpose(0, 2, 1, 3, 4).reshape(width, -1)

    w_q = by_pairs(np.asarray(inputs["L0_cond_Wq"])).T
    w_o = by_pairs(np.asarray(inputs["L0_cond_Wo"]).T)
    w_kd = np.asarray(inputs["L0_cond_Wkd"]).T
    w_kv = np.concatenate([np.asarray(inputs["L0_cond_Wku"]).T, np.asarray(inputs["L0_cond_Wvu"]).T], axis=1)
    w_ada = np.asarray(inputs["L0_cond_W_ada"])
    per = width // LATENT
    arrays = {
        "in_x": x,
        "in_cond_t": np.asarray(inputs["cond_2048"]).reshape(rows, tiles, P).transpose(2, 1, 0),
        "in_w_ada": w_ada.reshape(2 * tiles, P, tiles, P).transpose(0, 3, 2, 1).reshape(2 * tiles, P, width),
        "in_b_ada": np.asarray(inputs["L0_cond_b_ada"]).reshape(2 * tiles, P).T,
        "in_w_q": w_q.reshape(tiles, P, width),
        "in_w_kd": w_kd.reshape(tiles // per, per, P, LATENT).transpose(0, 2, 1, 3).reshape(tiles // per, P, width),
        "in_w_kv": w_kv.reshape(LATENT // P, P, 2 * LATENT).transpose(1, 0, 2),
        "in_w_o": w_o.reshape(tiles, P, width),
        "in_rope": rope_tables(tokens),
    }
    arrays = {n: np.ascontiguousarray(a) for n, a in arrays.items()}
    nc = bacc.Bacc("TRN2", target_bir_lowering=False, num_devices=1)
    args = [nc.dram_tensor(n, a.shape, mybir.dt.from_np(a.dtype), kind="ExternalInput").ap()
            for n, a in arrays.items()]
    args.append(nc.dram_tensor("out_y", x.shape, F32, kind="ExternalOutput").ap())
    adaln_gqa_attention(nc, *args)
    return run_bass_kernel_spmd(nc, [arrays], core_ids=[0]).results[0]["out_y"]
```

```python
from contextlib import ExitStack

import concourse.bass as bass
from concourse import mybir

ALU = mybir.AluOpType
ACT = mybir.ActivationFunctionType
AX = mybir.AxisListType
F32 = mybir.dt.float32
F32R = mybir.dt.float32r

P = 128
HEAD = 64
HALF = HEAD // 2
KV = 4
PER_KV = 4
LATENT = 256
LN_EPS = 1e-5
RING = 4

PASSES = ((0, 0), (0, 1), (1, 0))
PARTS = 2


def adaln_gqa_attention(nc: bass.Bass, x, cond_t, w_ada, b_ada, w_q, w_kd, w_kv, w_o, rope, out):
    B, T, C = x.shape
    KC = C // P
    KL = LATENT // P
    N2 = C // 2
    ADA = 2 * KC
    assert T == P and N2 == 512 and KV * PER_KV * HEAD == C and B == HEAD
    mod_dram = nc.dram_tensor("modulation", [P, B, ADA], F32, kind="Internal").ap()

    ctx = ExitStack()
    with ctx:
        def sb(name, shape, dt=F32):
            return ctx.enter_context(nc.sbuf_tensor(name, shape, dt))

        def bank(name):
            return ctx.enter_context(nc.psum_tensor(name, [P, 512], F32))

        def sem(name):
            return ctx.enter_context(nc.semaphore(name))

        wq = sb("wq", [P, PARTS, KC, C], F32R)
        wo = sb("wo", [P, PARTS, KC, C], F32R)
        wkd = sb("wkd", [P, PARTS, KC, LATENT], F32R)
        wkv = sb("wkv", [P, PARTS, KL, 2 * LATENT], F32R)
        ident = sb("ident", [P, P])
        tables = sb("tables", [P, 2, HEAD])
        minus_half = sb("minus_half", [P, 1])

        xs = sb("xs", [P, C])
        stats = sb("stats", [P, 2, 6])
        mean_var = sb("mean_var", [P, 2])
        var_eps = sb("var_eps", [P, 1])
        rstd = sb("rstd", [P, 1])
        mod = sb("mod", [P, ADA])
        ht = sb("ht", [P, PARTS, KC, P], F32R)
        q_nat = sb("q_nat", [P, C])
        h_st = q_nat[:, :].rearrange("p (k t) -> p k t", t=P)
        turned = sb("turned", [P, N2])
        ckv = turned[:, 0:LATENT]
        ckvt = sb("ckvt", [P, PARTS, KL, P], F32R)
        k_nat = sb("k_nat", [P, LATENT])
        kt = sb("kt", [P, PARTS, 2, 2 * P], F32R)
        v = sb("v", [P, LATENT])
        neg_max = sb("neg_max", [P, KV * PER_KV])
        sums = sb("sums", [P, KV * PER_KV])
        inv_sums = sb("inv_sums", [P, KV * PER_KV])

        with ExitStack() as early:
            cond = early.enter_context(nc.sbuf_tensor("cond", [P, KC, B], F32))
            ada_nat = early.enter_context(nc.sbuf_tensor("ada_nat", [P, 2, N2], F32))
            bias = early.enter_context(nc.sbuf_tensor("bias", [P, ADA], F32))
        qt = sb("qt", [P, PARTS, KC, P], F32R)
        with ExitStack() as early:
            mod_all = early.enter_context(nc.sbuf_tensor("mod_all", [P, B, ADA], F32))
        probs = sb("probs", [P, PER_KV, 2, P])
        with ExitStack() as early:
            ring = early.enter_context(nc.sbuf_tensor("ring", [P, RING, C], F32))
        pt = sb("pt", [P, 2, PER_KV * P])
        yt = sb("yt", [P, PARTS, 2, PER_KV, P], F32R)
        res = sb("res", [P, C])

        A, Bk, Cb, D, E, F, G, H = (bank(f"bank_{n}") for n in "abcdefgh")
        Q_BANK = (A, Bk)
        S_BANK = (E, F)
        Y_BANK = (G, H)

        const_loaded = sem("const_loaded")
        mod_stored = sem("mod_stored")
        mod_loaded = sem("mod_loaded")
        chunk_loaded = [sem(f"chunk_loaded{n}") for n in range(RING)]
        x_loaded = sem("x_loaded")
        res_loaded = sem("res_loaded")
        out_stored = sem("out_stored")
        ident_zero = sem("ident_zero")
        ident_ready = sem("ident_ready")
        ada_done = sem("ada_done")
        ada_copied = sem("ada_copied")
        ada_turned = sem("ada_turned")
        mod_biased = sem("mod_biased")
        mod_ready = sem("mod_ready")
        kt_zeroed = sem("kt_zeroed")
        ckvt_hi = sem("ckvt_hi")
        kt_hi = sem("kt_hi")
        qt_hi = sem("qt_hi")
        hi_split = sem("hi_split")
        lo_split = sem("lo_split")
        xt_done = sem("xt_done")
        ckv_done = sem("ckv_done")
        ckvt_done = sem("ckvt_done")
        q_done = sem("q_done")
        kv_done = sem("kv_done")
        kt_done = sem("kt_done")
        qt_done = sem("qt_done")
        s_done = sem("s_done")
        pt_done = sem("pt_done")
        pv_done = sem("pv_done")
        out_done = sem("out_done")
        half_stats = sem("half_stats")
        mean_done = sem("mean_done")
        rstd_ready = sem("rstd_ready")
        var_ready = sem("var_ready")
        half_set = sem("half_set")
        xn_ready = sem("xn_ready")
        h_lower = sem("h_lower")
        h_upper = sem("h_upper")
        h_hi = sem("h_hi")
        ht_ready = sem("ht_ready")
        ckv_ready = sem("ckv_ready")
        ckvt_ready = sem("ckvt_ready")
        q_times_table = sem("q_times_table")
        q_ready = sem("q_ready")
        k_times_table = sem("k_times_table")
        k_ready = sem("k_ready")
        kt_ready = sem("kt_ready")
        qt_ready = sem("qt_ready")
        v_ready = sem("v_ready")
        max_ready = sem("max_ready")
        exp_done = sem("exp_done")
        inv_ready = sem("inv_ready")
        probs_ready = sem("probs_ready")
        pt_ready = sem("pt_ready")
        y_hi = sem("y_hi")
        y_ready = sem("y_ready")
        out_added = sem("out_added")

        N_KD, N_Q, N_KVW, N_O = KC * LATENT // C, KC, 1, KC
        KD0, Q0 = ADA, ADA + N_KD
        KVW0 = Q0 + N_Q
        O0 = KVW0 + N_KVW
        CHUNKS = O0 + N_O
        SPLIT_ALL = CHUNKS - ADA

        def split_of(n):
            if n < Q0:
                per = C // LATENT
                k = (n - KD0) * per
                return lambda part: wkd[:, part, k:k + per, :].rearrange("p k n -> p (k n)")
            if n < KVW0:
                return lambda part: wq[:, part, n - Q0, :]
            if n < O0:
                return lambda part: wkv[:, part, :, :].rearrange("p k n -> p (k n)")
            return lambda part: wo[:, part, n - O0, :]

        def again(b):
            return not (isinstance(b, int) and b == 0)

        block = ctx.enter_context(nc.Block())

        @block.sync
        def _(sp):
            def load_x(b):
                if again(b):
                    sp.wait_ge(xt_done, 2 * b)
                sp.dma_start(xs[:, :], x[bass.ds(b, 1), :, :].rearrange("a t c -> (a t) c")
                             ).then_inc(x_loaded, 16)

            def load_chunk(n):
                slot, turn = n % RING, n // RING
                if turn:
                    old = n - RING
                    if old < ADA:
                        sp.wait_ge(ada_done, old + 1)
                    else:
                        sp.wait_ge(lo_split, old - ADA + 1)
                sp.dma_start(ring[:, slot, :], chunk_src(n)).then_inc(chunk_loaded[slot], 16)

            def chunk_src(n):
                if n < KD0:
                    return w_ada[n, :, :]
                if n < Q0:
                    return w_kd[n - KD0, :, :]
                if n < KVW0:
                    return w_q[n - Q0, :, :]
                if n < O0:
                    return w_kv
                return w_o[n - O0, :, :]

            load_x(0)
            sp.dma_start(cond[:, :, :], cond_t).then_inc(const_loaded, 16)
            sp.dma_start(bias[:, :], b_ada).then_inc(const_loaded, 16)
            sp.dma_start(tables[:, :, :], rope).then_inc(const_loaded, 16)
            for n in range(KD0):
                load_chunk(n)
            load_x(1)
            for n in range(KD0, O0):
                load_chunk(n)
            sp.wait_ge(mod_ready, 2)
            sp.dma_start(mod_dram, mod_all[:, :, :]).then_inc(mod_stored, 16)
            for n in range(O0, O0 + RING):
                load_chunk(n)
            load_x(2)
            for n in range(O0 + RING, CHUNKS):
                load_chunk(n)
            sp.wait_ge(mod_stored, 16)

            def load_mod(b):
                sp.wait_ge(h_lower, b)
                sp.wait_ge(h_upper, b)
                sp.dma_start(mod[:, :], mod_dram[:, bass.ds(b, 1), :].rearrange("p a m -> p (a m)")
                             ).then_inc(mod_loaded, 16)

            def slot(i, nxt, nxt2, third=True):
                if nxt2:
                    load_mod(i + 2)
                if again(i):
                    sp.wait_ge(out_stored, 32 * i)
                else:
                    sp.wait_ge(lo_split, SPLIT_ALL)
                sp.dma_start(res[:, :], x[bass.ds(i, 1), :, :].rearrange("a t c -> (a t) c")
                             ).then_inc(res_loaded, 16)
                if nxt2 and third:
                    load_x(i + 3)
                for n in range(2):
                    sp.wait_ge(out_added, 2 * i + n + 1)
                    sp.dma_start(out[bass.ds(i, 1), :, n * N2:(n + 1) * N2].rearrange("a t c -> (a t) c"),
                                 res[:, n * N2:(n + 1) * N2]).then_inc(out_stored, 16)

            slot(0, True, True)
            with sp.Fori(1, B - 3) as i:
                slot(i, True, True)
            slot(B - 3, True, True, third=False)
            slot(B - 2, True, False)
            slot(B - 1, False, False)
            sp.wait_ge(out_stored, 32 * B)

        @block.tensor
        def _(pe):
            def x_transposes(b):
                pe.wait_ge(xn_ready, b + 1)
                for half in range(2):
                    for k in range(4):
                        c = 4 * half + k
                        mm = pe.transpose(S_BANK[half][:, k * P:(k + 1) * P], xs[:, c * P:(c + 1) * P],
                                          ident[:, :])
                    mm.then_inc(xt_done, 1)

            def adaln(n):
                pe.wait_ge(chunk_loaded[n % RING], 16 * (n // RING + 1))
                k = n % KC
                for half in range(2):
                    mm = pe.matmul(Y_BANK[n // KC][half * B:(half + 1) * B, :], cond[:, k, :],
                                   ring[:, n % RING, half * N2:(half + 1) * N2],
                                   start=(k == 0), stop=(k == KC - 1))
                mm.then_inc(ada_done, 1)

            def ada_transposes(a):
                pe.wait_ge(ada_copied, a + 1)
                for j in range(4):
                    mm = pe.transpose(Q_BANK[a][:, j * P:(j + 1) * P], ada_nat[:, a, j * P:(j + 1) * P],
                                      ident[:, :])
                mm.then_inc(ada_turned, 1)

            def split_product(bank_ap, stationary, moving, ks, n_k):
                for k in ks:
                    for s, m in PASSES:
                        mm = pe.matmul(bank_ap, stationary(s, k), moving(m, k),
                                       start=(k == 0 and (s, m) == PASSES[0]),
                                       stop=(k == n_k - 1 and (s, m) == PASSES[-1]))
                return mm

            def ckv_product(b):
                pe.wait_ge(ht_ready, 2 * b + 2)
                if again(b):
                    pe.wait_ge(v_ready, b)
                split_product(Cb[:, 0:LATENT], lambda s, k: ht[:, s, k, :],
                              lambda m, k: wkd[:, m, k, :], range(KC), KC).then_inc(ckv_done, 1)

            def q_product(b, n, ks):
                if again(b) and 0 in ks:
                    pe.wait_ge(qt_ready, 2 * (b - 1) + n + 1)
                mm = split_product(Q_BANK[n][:, :], lambda s, k: ht[:, s, k, :],
                                   lambda m, k: wq[:, m, k, n * N2:(n + 1) * N2], ks, KC)
                if KC - 1 in ks:
                    mm.then_inc(q_done, 1)

            def ckv_transposes(b):
                pe.wait_ge(ckv_ready, b + 1)
                if again(b):
                    pe.wait_ge(kt_ready, b)
                for k in range(KL):
                    mm = pe.transpose(D[:, k * P:(k + 1) * P], ckv[:, k * P:(k + 1) * P], ident[:, :])
                mm.then_inc(ckvt_done, 1)

            def kv_product(b):
                pe.wait_ge(ckvt_ready, b + 1)
                split_product(Cb[:, :], lambda s, k: ckvt[:, s, k, :], lambda m, k: wkv[:, m, k, :],
                              range(KL), KL).then_inc(kv_done, 1)

            def k_transposes(b):
                pe.wait_ge(k_ready, b + 1)
                for p in range(2):
                    mm = pe.transpose(D[:, p * P:(p + 1) * P], k_nat[:, p * P:(p + 1) * P], ident[:, :])
                mm.then_inc(kt_done, 1)

            def q_transposes(b, n):
                pe.wait_ge(q_ready, 2 * b + n + 1)
                for j in range(4):
                    c = 4 * n + j
                    mm = pe.transpose(Q_BANK[n][:, j * P:(j + 1) * P], q_nat[:, c * P:(c + 1) * P],
                                      ident[:, :])
                mm.then_inc(qt_done, 1)

            def scores(b, p):
                pe.wait_ge(qt_ready, 2 * b + p + 1)
                if p == 0:
                    pe.wait_ge(kt_ready, b + 1)
                else:
                    pe.wait_ge(pt_ready, 4 * b + 2)
                for j in range(PER_KV):
                    for s, m in PASSES:
                        mm = pe.matmul(S_BANK[j // 2][:, (j % 2) * 2 * P:(j % 2 + 1) * 2 * P],
                                       qt[:, s, 4 * p + j, :], kt[:, m, p, :],
                                       start=((s, m) == PASSES[0]), stop=((s, m) == PASSES[-1]))
                    if j % 2:
                        mm.then_inc(s_done, 1)

            def p_transposes(b, p):
                pe.wait_ge(probs_ready, 4 * b + 2 * p + 2)
                for side in range(2):
                    for j in range(PER_KV):
                        mm = pe.transpose(S_BANK[side][:, j * P:(j + 1) * P], probs[:, j, side, :],
                                          ident[:, :])
                    mm.then_inc(pt_done, 1)

            def pv_product(b, p):
                if p == 0:
                    pe.wait_ge(v_ready, b + 1)
                if again(b):
                    pe.wait_ge(out_added, 2 * b - 1 + p)
                for side in range(2):
                    pe.wait_ge(pt_ready, 4 * b + 2 * p + side + 1)
                    g = 2 * p + side
                    pe.matmul(Y_BANK[p][side * HEAD:(side + 1) * HEAD, :], v[:, g * HEAD:(g + 1) * HEAD],
                              pt[:, side, :], start=True, stop=True).then_inc(pv_done, 1)

            def out_product(b, n, ks):
                if n == 0 and ks[0] % 4 == 0:
                    pe.wait_ge(y_ready, 2 * b + ks[0] // 4 + 1)
                mm = split_product(Y_BANK[n][:, :], lambda s, c: yt[:, s, c // 4, c % 4, :],
                                   lambda m, c: wo[:, m, c, n * N2:(n + 1) * N2], ks, KC)
                if KC - 1 in ks:
                    mm.then_inc(out_done, 1)

            pe.wait_ge(ident_ready, 1)
            x_transposes(0)
            pe.wait_ge(const_loaded, 48)
            for n in range(ADA):
                adaln(n)
            for a in range(2):
                ada_transposes(a)
            pe.wait_ge(lo_split, N_KD)
            ckv_product(0)
            pe.wait_ge(mod_ready, 2)
            for k in range(KC):
                pe.wait_ge(lo_split, N_KD + k + 1)
                q_product(0, 0, [k])
            ckv_transposes(0)
            q_product(0, 1, range(KC))
            pe.wait_ge(lo_split, N_KD + N_Q + N_KVW)
            kv_product(0)
            k_transposes(0)
            q_transposes(0, 0)
            q_transposes(0, 1)
            pe.wait_ge(h_lower, 1)
            pe.wait_ge(h_upper, 1)
            x_transposes(1)
            pe.wait_ge(h_lower, 2)
            pe.wait_ge(h_upper, 2)
            scores(0, 0)

            def slot(i, nxt, nxt2):
                if nxt:
                    ckv_product(i + 1)
                    q_product(i + 1, 0, range(0, 4))
                    ckv_transposes(i + 1)
                    q_product(i + 1, 0, range(4, 8))
                p_transposes(i, 0)
                if nxt:
                    kv_product(i + 1)
                scores(i, 1)
                pv_product(i, 0)
                if nxt:
                    q_product(i + 1, 1, range(KC))
                    k_transposes(i + 1)
                    q_transposes(i + 1, 0)
                p_transposes(i, 1)
                if not again(i):
                    pe.wait_ge(lo_split, SPLIT_ALL)
                out_product(i, 0, range(0, 2))
                pv_product(i, 1)
                out_product(i, 0, range(2, 4))
                if nxt:
                    q_transposes(i + 1, 1)
                if nxt2:
                    x_transposes(i + 2)
                out_product(i, 0, range(4, 8))
                out_product(i, 1, range(KC))
                if nxt2:
                    pe.wait_ge(h_lower, i + 3)
                    pe.wait_ge(h_upper, i + 3)
                if nxt:
                    scores(i + 1, 0)

            slot(0, True, True)
            with pe.Fori(1, B - 2) as i:
                slot(i, True, True)
            slot(B - 2, True, False)
            slot(B - 1, False, False)

        @block.scalar
        def _(act):
            def split_hi(n):
                act.wait_ge(chunk_loaded[n % RING], 16 * (n // RING + 1))
                act.activation(split_of(n)(0), ring[:, n % RING, :], ACT.Copy).then_inc(hi_split, 1)

            def exps(b, e):
                act.wait_ge(max_ready, 4 * b + e + 1)
                if again(b) or e >= 2:
                    act.wait_ge(pt_done, 4 * b + 2 * (e // 2))
                if again(b):
                    act.wait_ge(inv_ready, 2 * (b - 1) + e // 2 + 1)
                for r in range(4):
                    n = 4 * e + r
                    ex = act.activation(probs[:, 2 * (e % 2) + r // 2, r % 2, :],
                                        S_BANK[e % 2][:, r * P:(r + 1) * P], ACT.Exp,
                                        bias=neg_max[:, n:n + 1], accum_out=sums[:, n:n + 1])
                ex.then_inc(exp_done, 1)

            def split_kt_hi(b):
                act.wait_ge(kt_done, b + 1)
                for side in range(2):
                    rows = slice(side * HEAD, (side + 1) * HEAD)
                    hi = act.activation(kt[rows, 0, :, side * P:(side + 1) * P],
                                        D[rows, 0:2 * P].rearrange("d (p s) -> d p s", s=P), ACT.Copy)
                hi.then_inc(kt_hi, 1)

            def split_qt_hi(b, n):
                act.wait_ge(qt_done, 2 * b + n + 1)
                act.activation(qt[:, 0, 4 * n:4 * n + 4, :], Q_BANK[n][:, :], ACT.Copy).then_inc(qt_hi, 1)

            def copy_v(b):
                act.wait_ge(k_times_table, b + 1)
                if again(b):
                    act.wait_ge(pv_done, 4 * b)
                act.activation(v[:, :], Cb[:, LATENT:2 * LATENT], ACT.Copy).then_inc(v_ready, 1)

            def copy_pt(b, p, side):
                act.wait_ge(pt_done, 4 * b + 2 * p + side + 1)
                if again(b) or p:
                    act.wait_ge(pv_done, 4 * b + 2 * p + side - 1)
                act.activation(pt[:, side, :], S_BANK[side][:, :], ACT.Copy).then_inc(pt_ready, 1)

            def split_y_hi(b, p):
                act.wait_ge(pv_done, 4 * b + 2 * p + 2)
                if again(b):
                    act.wait_ge(out_done, 2 * b)
                act.activation(yt[:, 0, p, :, :], Y_BANK[p][:, :], ACT.Copy).then_inc(y_hi, 1)

            def modulate_lower(b, scale, shift):
                act.wait_ge(xt_done, 2 * b + 1)
                for k in range(4):
                    h = act.activation(h_st[:, k, :], E[:, k * P:(k + 1) * P], ACT.Identity,
                                       scale=scale(k), bias=shift(k))
                h.then_inc(h_lower, 1)

            act.wait_ge(mod_ready, 2)
            modulate_lower(0, lambda k: mod_all[:, 0, k:k + 1], lambda k: mod_all[:, 0, KC + k:KC + k + 1])
            for n in range(KD0, O0):
                split_hi(n)
            act.wait_ge(kt_zeroed, 1)
            split_kt_hi(0)
            split_qt_hi(0, 0)
            split_qt_hi(0, 1)
            copy_v(0)
            act.wait_ge(ht_ready, 2)
            modulate_lower(1, lambda k: mod_all[:, 1, k:k + 1], lambda k: mod_all[:, 1, KC + k:KC + k + 1])
            act.wait_ge(mod_stored, 16)

            def slot(i, nxt, nxt2):
                exps(i, 0)
                exps(i, 1)
                if not again(i):
                    for n in range(O0, CHUNKS):
                        split_hi(n)
                    act.wait_ge(lo_split, SPLIT_ALL)
                copy_pt(i, 0, 0)
                copy_pt(i, 0, 1)
                exps(i, 2)
                exps(i, 3)
                split_y_hi(i, 0)
                if nxt:
                    split_kt_hi(i + 1)
                    split_qt_hi(i + 1, 0)
                copy_pt(i, 1, 0)
                copy_pt(i, 1, 1)
                split_y_hi(i, 1)
                if nxt:
                    split_qt_hi(i + 1, 1)
                    copy_v(i + 1)
                if nxt2:
                    act.wait_ge(mod_loaded, 16 * (i + 1))
                    modulate_lower(i + 2, lambda k: mod[:, k:k + 1], lambda k: mod[:, KC + k:KC + k + 1])

            slot(0, True, True)
            with act.Fori(1, B - 2) as i:
                slot(i, True, True)
            slot(B - 2, True, False)
            slot(B - 1, False, False)

        @block.vector
        def _(dve):
            def row_stats(b):
                dve.wait_ge(x_loaded, 16 * (b + 1))
                for n in range(2):
                    dve.bn_stats(stats[:, n, :], xs[:, n * N2:(n + 1) * N2]).then_inc(half_stats, 1)

            def mean_and_variance(b):
                dve.bn_aggr(mean_var[:, :], stats[:, :, :].rearrange("p a s -> p (a s)")
                            ).then_inc(mean_done, 1)
                dve.wait_ge(mean_done, b + 1)
                dve.tensor_scalar(var_eps[:, :], mean_var[:, 1:2], LN_EPS, None, ALU.add
                                  ).then_inc(var_ready, 1)

            def normalise(b):
                dve.wait_ge(rstd_ready, b + 1)
                dve.tensor_scalar(xs[:, :], xs[:, :], mean_var[:, 0:1], rstd[:, 0:1],
                                  ALU.subtract, ALU.mult).then_inc(xn_ready, 1)

            def copy_ada(a):
                dve.wait_ge(ada_done, KC * (a + 1))
                dve.tensor_copy(ada_nat[:, a, :], Y_BANK[a][:, :]).then_inc(ada_copied, 1)

            def add_ada_bias(a):
                dve.wait_ge(ada_turned, a + 1)
                place = mod_all[:, :, a * KC:(a + 1) * KC].rearrange("p b (h j) -> p h j b", h=2)
                dve.tensor_tensor(place, Q_BANK[a][:, :].rearrange("p (j h b) -> p h j b", h=2, b=B),
                                  bias[:, a * KC:(a + 1) * KC].rearrange("p (h j o) -> p h j o", h=2, o=1)
                                  .broadcast_to([P, 2, 4, B]), ALU.add
                                  ).then_inc(mod_biased if a == 0 else mod_ready, 1)
                if a == 0:
                    dve.wait_ge(mod_biased, 1)
                    dve.tensor_scalar(mod_all[:, :, 0:KC], mod_all[:, :, 0:KC], 1.0, None, ALU.add
                                      ).then_inc(mod_ready, 1)

            def split_lo(n):
                dve.wait_ge(hi_split, n - ADA + 1)
                dve.tensor_tensor(split_of(n)(1), ring[:, n % RING, :], split_of(n)(0).bitcast(F32),
                                  ALU.subtract).then_inc(lo_split, 1)

            def modulate_upper(b, scale, shift):
                dve.wait_ge(xt_done, 2 * b + 2)
                for k in range(4, 8):
                    h = dve.tensor_scalar(h_st[:, k, :], F[:, (k - 4) * P:(k - 3) * P],
                                          scale(k), shift(k), ALU.mult, ALU.add)
                h.then_inc(h_upper, 1)

            def split_h(b):
                if again(b):
                    dve.wait_ge(q_done, 2 * b)
                for half in range(2):
                    if half == 0:
                        dve.wait_ge(h_lower, b + 1)
                    else:
                        dve.wait_ge(h_upper, b + 1)
                    ks = slice(4 * half, 4 * half + 4)
                    dve.tensor_copy(ht[:, 0, ks, :], h_st[:, ks, :]).then_inc(h_hi, 1)
                for half in range(2):
                    ks = slice(4 * half, 4 * half + 4)
                    dve.wait_ge(h_hi, 2 * b + half + 1)
                    dve.tensor_tensor(ht[:, 1, ks, :], h_st[:, ks, :], ht[:, 0, ks, :].bitcast(F32),
                                      ALU.subtract).then_inc(ht_ready, 1)

            def copy_ckv(b):
                dve.wait_ge(ckv_done, b + 1)
                if again(b):
                    dve.wait_ge(q_ready, 2 * b)
                dve.tensor_copy(ckv, Cb[:, 0:LATENT]).then_inc(ckv_ready, 1)

            def split_ckvt(b):
                dve.wait_ge(ckvt_done, b + 1)
                src = D[:, 0:LATENT].rearrange("p (k t) -> p k t", t=P)
                dve.tensor_copy(ckvt[:, 0, :, :], src).then_inc(ckvt_hi, 1)
                dve.wait_ge(ckvt_hi, b + 1)
                dve.tensor_tensor(ckvt[:, 1, :, :], src, ckvt[:, 0, :, :].bitcast(F32), ALU.subtract
                                  ).then_inc(ckvt_ready, 1)

            def split_kt_lo(b):
                dve.wait_ge(kt_hi, b + 1)
                for side in range(2):
                    rows, cols = slice(side * HEAD, (side + 1) * HEAD), slice(side * P, (side + 1) * P)
                    lo = dve.tensor_tensor(kt[rows, 1, :, cols],
                                           D[rows, 0:2 * P].rearrange("d (p s) -> d p s", s=P),
                                           kt[rows, 0, :, cols].bitcast(F32), ALU.subtract)
                lo.then_inc(kt_ready, 1)

            def split_qt_lo(b, n):
                dve.wait_ge(qt_hi, 2 * b + n + 1)
                cs = slice(4 * n, 4 * n + 4)
                dve.tensor_tensor(qt[:, 1, cs, :], Q_BANK[n][:, :].rearrange("p (j t) -> p j t", t=P),
                                  qt[:, 0, cs, :].bitcast(F32), ALU.subtract).then_inc(qt_ready, 1)

            def heads(ap):
                return ap.rearrange("p (h d) -> p h d", d=HEAD)

            def turn(src, straight, factor, signal):
                n = heads(src).shape[1]
                dve.scalar_tensor_tensor(heads(straight), heads(src), factor,
                                         tables[:, 0:1, :].broadcast_to([P, n, HEAD]), ALU.mult, ALU.mult)
                for a in range(2):
                    mine, other = slice(a * HALF, (a + 1) * HALF), slice((1 - a) * HALF, (2 - a) * HALF)
                    last = dve.scalar_tensor_tensor(
                        heads(turned[:, 0:n * HEAD])[:, :, mine], heads(src)[:, :, other], factor,
                        tables[:, 1:2, mine].broadcast_to([P, n, HALF]), ALU.mult, ALU.mult)
                last.then_inc(signal, 1)

            def turn_q(b, n):
                dve.wait_ge(q_done, 2 * b + n + 1)
                if n:
                    dve.wait_ge(k_ready, b + 1)
                turn(Q_BANK[n][:, :], q_nat[:, n * N2:(n + 1) * N2], 1.0, q_times_table)

            def turn_k(b):
                dve.wait_ge(kv_done, b + 1)
                dve.wait_ge(q_ready, 2 * b + 1)
                turn(Cb[:, 0:LATENT], k_nat[:, :], HEAD ** -0.5, k_times_table)

            def maxima(b, e):
                dve.wait_ge(s_done, 4 * b + e + 1)
                if again(b):
                    dve.wait_ge(exp_done, 4 * (b - 1) + e + 1)
                dve.tensor_reduce(neg_max[:, 4 * e:4 * e + 4],
                                  S_BANK[e % 2][:, :].rearrange("p (r s) -> p r s", s=P),
                                  AX.X, ALU.max, negate=True).then_inc(max_ready, 1)

            def invert(b, p):
                dve.wait_ge(exp_done, 4 * b + 2 * p + 2)
                if again(b):
                    dve.wait_ge(probs_ready, 4 * (b - 1) + 2 * p + 2)
                cols = slice(8 * p, 8 * p + 8)
                dve.reciprocal(inv_sums[:, cols], sums[:, cols]).then_inc(inv_ready, 1)

            def split_y_lo(b, p):
                dve.wait_ge(y_hi, 2 * b + p + 1)
                dve.tensor_tensor(yt[:, 1, p, :, :], Y_BANK[p][:, :].rearrange("p (j t) -> p j t", t=P),
                                  yt[:, 0, p, :, :].bitcast(F32), ALU.subtract).then_inc(y_ready, 1)

            def add_residual(b, n):
                dve.wait_ge(out_done, 2 * b + n + 1)
                if n == 0:
                    dve.wait_ge(res_loaded, 16 * (b + 1))
                cols = slice(n * N2, (n + 1) * N2)
                dve.tensor_tensor(res[:, cols], Y_BANK[n][:, :], res[:, cols], ALU.add
                                  ).then_inc(out_added, 1)

            row_stats(0)
            dve.wait_ge(half_stats, 2)
            mean_and_variance(0)
            normalise(0)
            dve.wait_ge(const_loaded, 48)
            copy_ada(0)
            copy_ada(1)
            add_ada_bias(0)
            add_ada_bias(1)
            dve.wait_ge(mod_ready, 2)
            modulate_upper(0, lambda k: mod_all[:, 0, k:k + 1], lambda k: mod_all[:, 0, KC + k:KC + k + 1])
            split_h(0)
            for n in range(KD0, Q0):
                split_lo(n)
            row_stats(1)
            dve.wait_ge(half_stats, 4)
            mean_and_variance(1)
            for n in range(Q0, O0):
                split_lo(n)
            normalise(1)
            copy_ckv(0)
            split_ckvt(0)
            turn_q(0, 0)
            turn_k(0)
            turn_q(0, 1)
            dve.wait_ge(kt_zeroed, 1)
            split_kt_lo(0)
            split_qt_lo(0, 0)
            split_qt_lo(0, 1)
            modulate_upper(1, lambda k: mod_all[:, 1, k:k + 1], lambda k: mod_all[:, 1, KC + k:KC + k + 1])
            split_h(1)

            def slot(i, nxt, nxt2):
                maxima(i, 0)
                maxima(i, 1)
                if nxt2:
                    row_stats(i + 2)
                    dve.wait_ge(half_stats, 2 * i + 6)
                if nxt:
                    copy_ckv(i + 1)
                if nxt2:
                    mean_and_variance(i + 2)
                invert(i, 0)
                if nxt:
                    split_ckvt(i + 1)
                if nxt2:
                    normalise(i + 2)
                if not again(i):
                    for n in range(O0, CHUNKS):
                        split_lo(n)
                if nxt:
                    turn_q(i + 1, 0)
                    turn_k(i + 1)
                maxima(i, 2)
                maxima(i, 3)
                invert(i, 1)
                split_y_lo(i, 0)
                if nxt:
                    turn_q(i + 1, 1)
                    split_kt_lo(i + 1)
                    split_qt_lo(i + 1, 0)
                split_y_lo(i, 1)
                if nxt:
                    split_qt_lo(i + 1, 1)
                if nxt2:
                    dve.wait_ge(mod_loaded, 16 * (i + 1))
                    modulate_upper(i + 2, lambda k: mod[:, k:k + 1], lambda k: mod[:, KC + k:KC + k + 1])
                    split_h(i + 2)
                add_residual(i, 0)
                add_residual(i, 1)

            slot(0, True, True)
            with dve.Fori(1, B - 2) as i:
                slot(i, True, True)
            slot(B - 2, True, False)
            slot(B - 1, False, False)

        @block.gpsimd
        def _(pool):
            def inverse_deviation(b):
                pool.wait_ge(var_ready, b + 1)
                pool.tensor_tensor(rstd[:, :], var_eps[:, :], minus_half[:, :], ALU.pow
                                   ).then_inc(rstd_ready, 1)

            def normalise_probs(b, e):
                if e % 2 == 0:
                    pool.wait_ge(inv_ready, 2 * b + e // 2 + 1)
                tiles = probs[:, 2 * (e % 2):2 * (e % 2) + 2, :, :].rearrange("p j h s -> p (j h) s")
                pool.tensor_tensor(tiles, tiles, inv_sums[:, 4 * e:4 * e + 4].rearrange("p (r o) -> p r o", o=1)
                                   .broadcast_to([P, 4, P]), ALU.mult).then_inc(probs_ready, 1)

            def add_q(b, n):
                pool.wait_ge(q_times_table, 2 * b + n + 1)
                cols = slice(n * N2, (n + 1) * N2)
                pool.tensor_tensor(q_nat[:, cols], q_nat[:, cols], turned[:, :], ALU.add
                                   ).then_inc(q_ready, 1)

            def add_k(b):
                pool.wait_ge(k_times_table, b + 1)
                pool.tensor_tensor(k_nat[:, :], k_nat[:, :], turned[:, 0:LATENT], ALU.add).then_inc(k_ready, 1)

            pool.memset(ident[:, :], 0.0).then_inc(ident_zero, 1)
            pool.wait_ge(ident_zero, 1)
            pool.affine_select(out=ident[:, :], in_=ident[:, :], compare_op=ALU.not_equal, fill=1.0,
                               base=0, pattern=[[-1, P]], channel_multiplier=1).then_inc(ident_ready, 1)
            pool.memset(minus_half[:, :], -0.5).then_inc(half_set, 1)
            pool.wait_ge(half_set, 1)
            inverse_deviation(0)
            pool.memset(kt[:, :, :, :].bitcast(F32), 0.0).then_inc(kt_zeroed, 1)
            inverse_deviation(1)
            add_q(0, 0)
            add_k(0)
            add_q(0, 1)

            def slot(i, nxt, nxt2):
                if nxt2:
                    inverse_deviation(i + 2)
                normalise_probs(i, 0)
                normalise_probs(i, 1)
                if nxt:
                    add_q(i + 1, 0)
                    add_k(i + 1)
                normalise_probs(i, 2)
                normalise_probs(i, 3)
                if nxt:
                    add_q(i + 1, 1)

            slot(0, True, True)
            with pool.Fori(1, B - 2) as i:
                slot(i, True, True)
            slot(B - 2, True, False)
            slot(B - 1, False, False)


def rope_tables(tokens):
    import numpy as np

    freqs = (np.float32(1.0) / np.float32(10000.0) ** (np.arange(0, HEAD, 2, dtype=np.float32)
                                                       / np.float32(HEAD))).astype(np.float32)
    emb = np.arange(tokens, dtype=np.float32)[:, None] * freqs[None, :]
    cos, sin = np.cos(emb), np.sin(emb)
    return np.ascontiguousarray(np.stack([np.concatenate([cos, cos], axis=-1),
                                          np.concatenate([-sin, sin], axis=-1)], axis=1), dtype=np.float32)


def kernel(**inputs):
    import numpy as np
    import concourse.bacc as bacc
    from concourse.bass_utils import run_bass_kernel_spmd

    x = np.ascontiguousarray(inputs["x"])
    rows, tokens, width = x.shape
    tiles = width // P

    def by_pairs(w):
        return w.reshape(KV // 2, 2, PER_KV, HEAD, -1).transpose(0, 2, 1, 3, 4).reshape(width, -1)

    w_q = by_pairs(np.asarray(inputs["L0_cond_Wq"])).T
    w_o = by_pairs(np.asarray(inputs["L0_cond_Wo"]).T)
    w_kd = np.asarray(inputs["L0_cond_Wkd"]).T
    w_kv = np.concatenate([np.asarray(inputs["L0_cond_Wku"]).T, np.asarray(inputs["L0_cond_Wvu"]).T], axis=1)
    w_ada = np.asarray(inputs["L0_cond_W_ada"])
    per = width // LATENT
    arrays = {
        "in_x": x,
        "in_cond_t": np.asarray(inputs["cond_2048"]).reshape(rows, tiles, P).transpose(2, 1, 0),
        "in_w_ada": w_ada.reshape(2, width, tiles, P).transpose(0, 2, 3, 1).reshape(2 * tiles, P, width),
        "in_b_ada": np.asarray(inputs["L0_cond_b_ada"]).reshape(2 * tiles, P).T,
        "in_w_q": w_q.reshape(tiles, P, width),
        "in_w_kd": w_kd.reshape(tiles // per, per, P, LATENT).transpose(0, 2, 1, 3).reshape(tiles // per, P, width),
        "in_w_kv": w_kv.reshape(LATENT // P, P, 2 * LATENT).transpose(1, 0, 2).reshape(P, width),
        "in_w_o": w_o.reshape(tiles, P, width),
        "in_rope": rope_tables(tokens),
    }
    arrays = {n: np.ascontiguousarray(a) for n, a in arrays.items()}
    nc = bacc.Bacc("TRN2", target_bir_lowering=False, num_devices=1)
    args = [nc.dram_tensor(n, a.shape, mybir.dt.from_np(a.dtype), kind="ExternalInput").ap()
            for n, a in arrays.items()]
    args.append(nc.dram_tensor("out_y", x.shape, F32, kind="ExternalOutput").ap())
    adaln_gqa_attention(nc, *args)
    return run_bass_kernel_spmd(nc, [arrays], core_ids=[0]).results[0]["out_y"]
```

```python
from contextlib import ExitStack

import concourse.bass as bass
from concourse import mybir

ALU = mybir.AluOpType
ACT = mybir.ActivationFunctionType
AX = mybir.AxisListType
F32 = mybir.dt.float32
F32R = mybir.dt.float32r

P = 128
HEAD = 64
HALF = HEAD // 2
KV = 4
PER_KV = 4
LATENT = 256
LN_EPS = 1e-5
RING = 4

PASSES = ((0, 0), (0, 1), (1, 0))
PARTS = 2


def adaln_gqa_attention(nc: bass.Bass, x, x_turned, cond_t, w_ada, b_ada, w_q, w_kd, w_kv, w_o, rope, out):
    B, T, C = x.shape
    KC = C // P
    KL = LATENT // P
    N2 = C // 2
    ADA = 2 * KC
    assert T == P and N2 == 512 and KV * PER_KV * HEAD == C and B == HEAD
    mod_dram = nc.dram_tensor("modulation", [P, B, ADA], F32, kind="Internal").ap()

    ctx = ExitStack()
    with ctx:
        def sb(name, shape, dt=F32):
            return ctx.enter_context(nc.sbuf_tensor(name, shape, dt))

        def bank(name):
            return ctx.enter_context(nc.psum_tensor(name, [P, 512], F32))

        def sem(name):
            return ctx.enter_context(nc.semaphore(name))

        wq = sb("wq", [P, PARTS, KC, C], F32R)
        wo = sb("wo", [P, PARTS, KC, C], F32R)
        wkd = sb("wkd", [P, PARTS, KC, LATENT], F32R)
        wkv = sb("wkv", [P, PARTS, KL, 2 * LATENT], F32R)
        ident = sb("ident", [P, P])
        tables = sb("tables", [P, 2, HEAD])
        minus_half = sb("minus_half", [P, 1])

        xt = sb("xt", [P, KC, P])
        mean_rstd = sb("mean_rstd", [P, 2, P])
        stats = sb("stats", [P, 2, 6])
        mean_var = sb("mean_var", [P, 2])
        var_eps = sb("var_eps", [P, 1])
        rstd = sb("rstd", [P, 1])
        mod = sb("mod", [P, ADA])
        ht = sb("ht", [P, PARTS, KC, P], F32R)
        q_nat = sb("q_nat", [P, C])
        xs = q_nat
        turned = sb("turned", [P, N2])
        ckv = turned[:, 0:LATENT]
        k_nat = turned[:, LATENT:2 * LATENT]
        ckvt = sb("ckvt", [P, PARTS, KL, P], F32R)
        kt = sb("kt", [P, PARTS, 2, 2 * P], F32R)
        v = sb("v", [P, LATENT])
        neg_max = sb("neg_max", [P, KV * PER_KV])
        sums = sb("sums", [P, KV * PER_KV])
        inv_sums = sb("inv_sums", [P, KV * PER_KV])

        with ExitStack() as early:
            cond = early.enter_context(nc.sbuf_tensor("cond", [P, KC, B], F32))
            ada_nat = early.enter_context(nc.sbuf_tensor("ada_nat", [P, 2, N2], F32))
            bias = early.enter_context(nc.sbuf_tensor("bias", [P, ADA], F32))
        qt = sb("qt", [P, PARTS, KC, P], F32R)
        with ExitStack() as early:
            mod_all = early.enter_context(nc.sbuf_tensor("mod_all", [P, B, ADA], F32))
        probs = sb("probs", [P, PER_KV, 2, P])
        with ExitStack() as early:
            ring = early.enter_context(nc.sbuf_tensor("ring", [P, RING, C], F32))
        pt = sb("pt", [P, 2, PER_KV * P])
        yt = sb("yt", [P, PARTS, 2, PER_KV, P], F32R)
        res = sb("res", [P, C])

        A, Bk, Cb, D, E, F, G, H = (bank(f"bank_{n}") for n in "abcdefgh")
        Q_BANK = (A, Bk)
        S_BANK = (E, F)
        STATS = D[:, LATENT:LATENT + 2 * P]
        Y_BANK = (G, H)

        def last_row(b):
            return isinstance(b, int) and b == B - 1

        def out_bank(b, n):
            return A if last_row(b) and n == 1 else Y_BANK[n]

        def s_bank(b, p, side):
            return (Cb, D)[side] if last_row(b) and p == 1 else S_BANK[side]

        def probs_of(b, p):
            return xt[:, :, :].rearrange("p (j h) s -> p j h s", h=2) if last_row(b) and p == 1 else probs

        const_loaded = sem("const_loaded")
        mod_stored = sem("mod_stored")
        mod_loaded = sem("mod_loaded")
        chunk_loaded = [sem(f"chunk_loaded{n}") for n in range(RING)]
        x_loaded = sem("x_loaded")
        res_loaded = sem("res_loaded")
        out_stored = sem("out_stored")
        ident_zero = sem("ident_zero")
        ident_ready = sem("ident_ready")
        ada_done = sem("ada_done")
        ada_copied = sem("ada_copied")
        ada_turned = sem("ada_turned")
        mod_biased = sem("mod_biased")
        mod_ready = sem("mod_ready")
        kt_zeroed = sem("kt_zeroed")
        ckvt_hi = sem("ckvt_hi")
        kt_hi = sem("kt_hi")
        qt_hi = sem("qt_hi")
        hi_split = sem("hi_split")
        lo_split = sem("lo_split")
        pool_split = sem("pool_split")
        xt_loaded = sem("xt_loaded")
        stats_turned = sem("stats_turned")
        stats_ready = sem("stats_ready")
        centred = sem("centred")
        ckv_done = sem("ckv_done")
        ckvt_done = sem("ckvt_done")
        q_done = sem("q_done")
        kv_done = sem("kv_done")
        kt_done = sem("kt_done")
        qt_done = sem("qt_done")
        s_done = sem("s_done")
        pt_done = sem("pt_done")
        pv_done = sem("pv_done")
        out_done = sem("out_done")
        half_stats = sem("half_stats")
        mean_done = sem("mean_done")
        rstd_ready = sem("rstd_ready")
        var_ready = sem("var_ready")
        half_set = sem("half_set")
        xn_ready = sem("xn_ready")
        h_lower = sem("h_lower")
        h_upper = sem("h_upper")
        h_hi = sem("h_hi")
        ht_ready = sem("ht_ready")
        ckv_ready = sem("ckv_ready")
        ckvt_ready = sem("ckvt_ready")
        q_times_table = sem("q_times_table")
        q_ready = sem("q_ready")
        k_times_table = sem("k_times_table")
        k_ready = sem("k_ready")
        kt_ready = sem("kt_ready")
        qt_ready = sem("qt_ready")
        v_ready = sem("v_ready")
        max_ready = sem("max_ready")
        exp_done = sem("exp_done")
        inv_ready = sem("inv_ready")
        probs_ready = sem("probs_ready")
        pt_ready = sem("pt_ready")
        y_hi = sem("y_hi")
        y_ready = sem("y_ready")
        out_added = sem("out_added")

        per = C // LATENT
        EARLY_Q = 2
        CHUNKS = ([("kd", k) for k in range(0, KC, per)] + [("kv", 0)] + [("q", k) for k in range(EARLY_Q)]
                  + [("ada", k) for k in range(ADA)] + [("q", k) for k in range(EARLY_Q, KC)]
                  + [("o", k) for k in range(KC)])
        SPLIT = [c for c in CHUNKS if c[0] != "ada"]
        POOLS = [("q", 2), ("q", 3), ("o", 1), ("o", 3)]
        LOWS = [c for c in SPLIT if c not in POOLS]

        def split_done(chunk):
            if chunk in POOLS:
                return pool_split, POOLS.index(chunk) + 1
            return lo_split, LOWS.index(chunk) + 1

        def ring_slot(chunk):
            return CHUNKS.index(chunk) % RING

        def left_ring(slots):
            return [split_done([c for c in CHUNKS if ring_slot(c) == slot][-1]) for slot in slots]

        def chunk_here(chunk):
            return chunk_loaded[ring_slot(chunk)], 16 * (CHUNKS.index(chunk) // RING + 1)

        def split_of(chunk):
            kind, k = chunk
            if kind == "kd":
                return lambda part: wkd[:, part, k:k + per, :].rearrange("p k n -> p (k n)")
            if kind == "kv":
                return lambda part: wkv[:, part, :, :].rearrange("p k n -> p (k n)")
            weight = wq if kind == "q" else wo
            return lambda part: weight[:, part, k, :]

        def again(b):
            return not (isinstance(b, int) and b == 0)

        block = ctx.enter_context(nc.Block())

        @block.sync
        def _(sp):
            def load_xt(b):
                if again(b):
                    sp.wait_ge(ht_ready, 2 * b)
                sp.dma_start(xt[:, :, :], x_turned[bass.ds(b, 1), :, :, :].rearrange("a p k t -> (a p) k t")
                             ).then_inc(xt_loaded, 16)

            def load_x(b):
                if not isinstance(b, int) or b > 2:
                    sp.wait_ge(qt_done, 2 * b - 2)
                elif b:
                    sp.wait_ge(half_stats, 2 * b)
                sp.dma_start(xs[:, :], x[bass.ds(b, 1), :, :].rearrange("a t c -> (a t) c")
                             ).then_inc(x_loaded, 16)

            def load_chunks(chunks):
                for chunk in chunks:
                    at = CHUNKS.index(chunk)
                    if at >= RING:
                        kind, k = CHUNKS[at - RING]
                        if kind == "ada":
                            sp.wait_ge(ada_done, k + 1)
                        else:
                            sp.wait_ge(*split_done((kind, k)))
                    sp.dma_start(ring[:, ring_slot(chunk), :], chunk_src(*chunk)
                                 ).then_inc(chunk_loaded[ring_slot(chunk)], 16)

            def chunk_src(kind, k):
                if kind == "kd":
                    return w_kd[k // per, :, :]
                if kind == "kv":
                    return w_kv
                return {"q": w_q, "ada": w_ada, "o": w_o}[kind][k, :, :]

            load_x(0)
            load_chunks(CHUNKS[:2])
            load_xt(0)
            load_chunks(CHUNKS[2:RING])
            sp.dma_start(cond[:, :, :], cond_t).then_inc(const_loaded, 16)
            sp.dma_start(bias[:, :], b_ada).then_inc(const_loaded, 16)
            sp.dma_start(tables[:, :, :], rope).then_inc(const_loaded, 16)
            late_q = CHUNKS.index(("q", EARLY_Q))
            load_chunks(CHUNKS[RING:late_q])
            load_x(1)
            load_chunks(CHUNKS[late_q:late_q + RING])
            load_xt(1)
            load_x(2)
            load_chunks(CHUNKS[late_q + RING:late_q + 2 * RING])
            sp.wait_ge(mod_ready, 2)
            sp.dma_start(mod_dram, mod_all[:, :, :]).then_inc(mod_stored, 16)
            load_chunks(CHUNKS[late_q + 2 * RING:])
            sp.wait_ge(mod_stored, 16)

            def load_mod(b):
                sp.wait_ge(h_lower, b)
                sp.wait_ge(h_upper, b)
                sp.dma_start(mod[:, :], mod_dram[:, bass.ds(b, 1), :].rearrange("p a m -> p (a m)")
                             ).then_inc(mod_loaded, 16)

            def slot(i, nxt, nxt2, third=True):
                if nxt2:
                    load_mod(i + 2)
                    load_xt(i + 2)
                if again(i):
                    sp.wait_ge(out_stored, 32 * i)
                else:
                    for last_split in left_ring((3,)):
                        sp.wait_ge(*last_split)
                sp.dma_start(res[:, :], x[bass.ds(i, 1), :, :].rearrange("a t c -> (a t) c")
                             ).then_inc(res_loaded, 16)
                if nxt2 and third:
                    load_x(i + 3)
                for n in range(2):
                    sp.wait_ge(out_added, 2 * i + n + 1)
                    sp.dma_start(out[bass.ds(i, 1), :, n * N2:(n + 1) * N2].rearrange("a t c -> (a t) c"),
                                 res[:, n * N2:(n + 1) * N2]).then_inc(out_stored, 16)

            slot(0, True, True)
            with sp.Fori(1, B - 3) as i:
                slot(i, True, True)
            slot(B - 3, True, True, third=False)
            slot(B - 2, True, False)
            slot(B - 1, False, False)
            sp.wait_ge(out_stored, 32 * B)

        @block.tensor
        def _(pe):
            def spread_stats(b):
                pe.wait_ge(rstd_ready, b + 1)
                if again(b):
                    pe.wait_ge(stats_ready, b)
                pe.transpose(STATS[:, 0:P], mean_var[:, 0:1].broadcast_to([P, P]), ident[:, :])
                pe.transpose(STATS[:, P:2 * P], rstd[:, 0:1].broadcast_to([P, P]), ident[:, :]
                             ).then_inc(stats_turned, 1)

            def adaln(n):
                pe.wait_ge(*chunk_here(("ada", n)))
                k = n % KC
                for half in range(2):
                    mm = pe.matmul(Y_BANK[n // KC][half * B:(half + 1) * B, :], cond[:, k, :],
                                   ring[:, ring_slot(("ada", n)), half * N2:(half + 1) * N2],
                                   start=(k == 0), stop=(k == KC - 1))
                mm.then_inc(ada_done, 1)

            def ada_transposes(a):
                pe.wait_ge(ada_copied, a + 1)
                for j in range(4):
                    mm = pe.transpose(Q_BANK[a][:, j * P:(j + 1) * P], ada_nat[:, a, j * P:(j + 1) * P],
                                      ident[:, :])
                mm.then_inc(ada_turned, 1)

            def split_product(bank_ap, stationary, moving, ks, n_k):
                for k in ks:
                    for s, m in PASSES:
                        mm = pe.matmul(bank_ap, stationary(s, k), moving(m, k),
                                       start=(k == 0 and (s, m) == PASSES[0]),
                                       stop=(k == n_k - 1 and (s, m) == PASSES[-1]))
                return mm

            def ckv_product(b):
                if again(b):
                    pe.wait_ge(v_ready, b)
                for half in range(2):
                    pe.wait_ge(ht_ready, 2 * b + half + 1)
                    mm = split_product(Cb[:, 0:LATENT], lambda s, k: ht[:, s, k, :],
                                       lambda m, k: wkd[:, m, k, :], range(4 * half, 4 * half + 4), KC)
                mm.then_inc(ckv_done, 1)

            def q_product(b, n, ks):
                if again(b) and 0 in ks:
                    pe.wait_ge(qt_ready, 2 * (b - 1) + n + 1)
                mm = split_product(Q_BANK[n][:, :], lambda s, k: ht[:, s, k, :],
                                   lambda m, k: wq[:, m, k, n * N2:(n + 1) * N2], ks, KC)
                if KC - 1 in ks:
                    mm.then_inc(q_done, 1)

            def ckv_transposes(b):
                pe.wait_ge(ckv_ready, b + 1)
                if again(b):
                    pe.wait_ge(kt_ready, b)
                for k in range(KL):
                    mm = pe.transpose(D[:, k * P:(k + 1) * P], ckv[:, k * P:(k + 1) * P], ident[:, :])
                mm.then_inc(ckvt_done, 1)

            def kv_product(b):
                pe.wait_ge(ckvt_ready, b + 1)
                split_product(Cb[:, :], lambda s, k: ckvt[:, s, k, :], lambda m, k: wkv[:, m, k, :],
                              range(KL), KL).then_inc(kv_done, 1)

            def k_transposes(b):
                pe.wait_ge(k_ready, b + 1)
                for p in range(2):
                    mm = pe.transpose(D[:, p * P:(p + 1) * P], k_nat[:, p * P:(p + 1) * P], ident[:, :])
                mm.then_inc(kt_done, 1)

            def q_transposes(b, n):
                pe.wait_ge(q_ready, 2 * b + n + 1)
                for j in range(4):
                    c = 4 * n + j
                    mm = pe.transpose(Q_BANK[n][:, j * P:(j + 1) * P], q_nat[:, c * P:(c + 1) * P],
                                      ident[:, :])
                mm.then_inc(qt_done, 1)

            def scores(b, p):
                pe.wait_ge(qt_ready, 2 * b + p + 1)
                if p == 0:
                    pe.wait_ge(kt_ready, b + 1)
                elif last_row(b):
                    pe.wait_ge(v_ready, b + 1)
                else:
                    pe.wait_ge(pt_ready, 4 * b + 2)
                for j in range(PER_KV):
                    for s, m in PASSES:
                        mm = pe.matmul(s_bank(b, p, j // 2)[:, (j % 2) * 2 * P:(j % 2 + 1) * 2 * P],
                                       qt[:, s, 4 * p + j, :], kt[:, m, p, :],
                                       start=((s, m) == PASSES[0]), stop=((s, m) == PASSES[-1]))
                    if j % 2:
                        mm.then_inc(s_done, 1)

            def p_transposes(b, p):
                pe.wait_ge(probs_ready, 4 * b + 2 * p + 2)
                for side in range(2):
                    for j in range(PER_KV):
                        mm = pe.transpose(s_bank(b, p, side)[:, j * P:(j + 1) * P], probs_of(b, p)[:, j, side, :],
                                          ident[:, :])
                    mm.then_inc(pt_done, 1)

            def pv_product(b, p):
                if p == 0:
                    pe.wait_ge(v_ready, b + 1)
                if again(b):
                    pe.wait_ge(out_added, 2 * b - 1 + p)
                for side in range(2):
                    pe.wait_ge(pt_ready, 4 * b + 2 * p + side + 1)
                    g = 2 * p + side
                    pe.matmul(Y_BANK[p][side * HEAD:(side + 1) * HEAD, :], v[:, g * HEAD:(g + 1) * HEAD],
                              pt[:, side, :], start=True, stop=True).then_inc(pv_done, 1)

            def out_product(b, n, ks):
                if n == 0 and ks[0] % 4 == 0:
                    pe.wait_ge(y_ready, 2 * b + ks[0] // 4 + 1)
                mm = split_product(out_bank(b, n)[:, :], lambda s, c: yt[:, s, c // 4, c % 4, :],
                                   lambda m, c: wo[:, m, c, n * N2:(n + 1) * N2], ks, KC)
                if KC - 1 in ks:
                    mm.then_inc(out_done, 1)

            pe.wait_ge(ident_ready, 1)
            spread_stats(0)
            pe.wait_ge(const_loaded, 48)
            for n in range(ADA):
                adaln(n)
                if n == KC + 2:
                    ada_transposes(0)
            ada_transposes(1)
            pe.wait_ge(*split_done(("kd", KC - per)))
            ckv_product(0)
            pe.wait_ge(mod_ready, 2)
            for k in range(4):
                pe.wait_ge(*split_done(("q", k)))
                q_product(0, 0, [k])
                q_product(0, 1, [k])
                if k == 0:
                    spread_stats(1)
                if k == 1:
                    pe.wait_ge(stats_ready, 2)
                    ckv_transposes(0)
            pe.wait_ge(*split_done(("kv", 0)))
            kv_product(0)
            for k in range(4, KC):
                pe.wait_ge(*split_done(("q", k)))
                q_product(0, 0, [k])
            k_transposes(0)
            q_product(0, 1, range(4, KC))
            q_transposes(0, 0)
            ckv_product(1)
            scores(0, 0)
            q_transposes(0, 1)

            def slot(i, nxt, nxt2):
                last = not nxt
                if nxt:
                    if again(i):
                        ckv_product(i + 1)
                    if nxt2:
                        spread_stats(i + 2)
                    q_product(i + 1, 0, range(0, 4))
                    if nxt2:
                        pe.wait_ge(stats_ready, i + 3)
                    ckv_transposes(i + 1)
                    q_product(i + 1, 0, range(4, 8))
                p_transposes(i, 0)
                if nxt:
                    kv_product(i + 1)
                    scores(i, 1)
                pv_product(i, 0)
                if nxt:
                    q_product(i + 1, 1, range(KC))
                    k_transposes(i + 1)
                    q_transposes(i + 1, 0)
                if last:
                    p_transposes(i, 1)
                    pv_product(i, 1)
                    out_product(i, 0, range(0, 4))
                    out_product(i, 1, range(0, 4))
                else:
                    p_transposes(i, 1)
                    if not again(i):
                        for chunk in (POOLS[-1], LOWS[-1]):
                            pe.wait_ge(*split_done(chunk))
                    out_product(i, 0, range(0, 2))
                    pv_product(i, 1)
                    out_product(i, 0, range(2, 4))
                if nxt:
                    q_transposes(i + 1, 1)
                if nxt:
                    scores(i + 1, 0)
                out_product(i, 0, range(4, 8))
                if nxt and last_row(i + 1):
                    scores(i + 1, 1)
                out_product(i, 1, range(4, 8) if last else range(KC))

            slot(0, True, True)
            with pe.Fori(1, B - 2) as i:
                slot(i, True, True)
            slot(B - 2, True, False)
            slot(B - 1, False, False)

        @block.scalar
        def _(act):
            def split_hi(chunk):
                act.wait_ge(*chunk_here(chunk))
                act.activation(split_of(chunk)(0), ring[:, ring_slot(chunk), :], ACT.Copy).then_inc(hi_split, 1)

            def exps(b, e):
                act.wait_ge(max_ready, 4 * b + e + 1)
                if last_row(b) and e >= 2:
                    act.wait_ge(ht_ready, 2 * b + 2)
                elif again(b) or e >= 2:
                    act.wait_ge(pt_done, 4 * b + 2 * (e // 2))
                if again(b):
                    act.wait_ge(inv_ready, 2 * (b - 1) + e // 2 + 1)
                for r in range(4):
                    n = 4 * e + r
                    ex = act.activation(probs_of(b, e // 2)[:, 2 * (e % 2) + r // 2, r % 2, :],
                                        s_bank(b, e // 2, e % 2)[:, r * P:(r + 1) * P], ACT.Exp,
                                        bias=neg_max[:, n:n + 1], accum_out=sums[:, n:n + 1])
                ex.then_inc(exp_done, 1)

            def split_kt_hi(b):
                act.wait_ge(kt_done, b + 1)
                for side in range(2):
                    rows = slice(side * HEAD, (side + 1) * HEAD)
                    hi = act.activation(kt[rows, 0, :, side * P:(side + 1) * P],
                                        D[rows, 0:2 * P].rearrange("d (p s) -> d p s", s=P), ACT.Copy)
                hi.then_inc(kt_hi, 1)

            def split_qt_hi(b, n):
                act.wait_ge(qt_done, 2 * b + n + 1)
                act.activation(qt[:, 0, 4 * n:4 * n + 4, :], Q_BANK[n][:, :], ACT.Copy).then_inc(qt_hi, 1)

            def copy_v(b):
                act.wait_ge(k_times_table, b + 1)
                if again(b):
                    act.wait_ge(pv_done, 4 * b)
                act.activation(v[:, :], Cb[:, LATENT:2 * LATENT], ACT.Copy).then_inc(v_ready, 1)

            def copy_pt(b, p, side):
                act.wait_ge(pt_done, 4 * b + 2 * p + side + 1)
                if again(b) or p:
                    act.wait_ge(pv_done, 4 * b + 2 * p + side - 1)
                act.activation(pt[:, side, :], s_bank(b, p, side)[:, :], ACT.Copy).then_inc(pt_ready, 1)

            def split_y_hi(b, p):
                act.wait_ge(pv_done, 4 * b + 2 * p + 2)
                if again(b):
                    act.wait_ge(out_done, 2 * b)
                act.activation(yt[:, 0, p, :, :], Y_BANK[p][:, :], ACT.Copy).then_inc(y_hi, 1)

            def modulate_lower(b, scale, shift):
                act.wait_ge(xn_ready, b + 1)
                for k in range(4):
                    h = act.activation(xt[:, k, :], xt[:, k, :], ACT.Identity,
                                       scale=scale(k), bias=shift(k))
                h.then_inc(h_lower, 1)

            def copy_stats(b):
                act.wait_ge(stats_turned, b + 1)
                if again(b):
                    act.wait_ge(xn_ready, b)
                act.activation(mean_rstd[:, :, :].rearrange("p a t -> p (a t)"), STATS, ACT.Copy
                               ).then_inc(stats_ready, 1)

            split_hi(SPLIT[0])
            copy_stats(0)
            for chunk in SPLIT[1:3 + EARLY_Q]:
                split_hi(chunk)
            act.wait_ge(mod_ready, 2)
            modulate_lower(0, lambda k: mod_all[:, 0, k:k + 1], lambda k: mod_all[:, 0, KC + k:KC + k + 1])
            for k in range(EARLY_Q, 6):
                split_hi(("q", k))
            copy_stats(1)
            split_hi(("q", 6))
            for chunk in (("q", 7), ("o", 0), ("o", 1)):
                split_hi(chunk)
            act.wait_ge(ht_ready, 2)
            modulate_lower(1, lambda k: mod_all[:, 1, k:k + 1], lambda k: mod_all[:, 1, KC + k:KC + k + 1])
            split_hi(("o", 2))
            copy_v(0)
            act.wait_ge(kt_zeroed, 1)
            split_kt_hi(0)
            split_hi(("o", 3))
            split_qt_hi(0, 0)
            split_hi(("o", 4))
            act.wait_ge(mod_stored, 16)

            def slot(i, nxt, nxt2):
                exps(i, 0)
                exps(i, 1)
                if not again(i):
                    split_qt_hi(0, 1)
                if nxt2:
                    copy_stats(i + 2)
                if not again(i):
                    for k in range(5, KC):
                        split_hi(("o", k))
                    for last_split in left_ring((0,)):
                        act.wait_ge(*last_split)
                if not nxt:
                    exps(i, 2)
                    exps(i, 3)
                copy_pt(i, 0, 0)
                copy_pt(i, 0, 1)
                if nxt:
                    exps(i, 2)
                    exps(i, 3)
                else:
                    copy_pt(i, 1, 0)
                    copy_pt(i, 1, 1)
                if nxt2:
                    act.wait_ge(mod_loaded, 16 * (i + 1))
                    modulate_lower(i + 2, lambda k: mod[:, k:k + 1], lambda k: mod[:, KC + k:KC + k + 1])
                if not again(i):
                    for last_split in left_ring((1, 2)):
                        act.wait_ge(*last_split)
                split_y_hi(i, 0)
                if nxt:
                    split_kt_hi(i + 1)
                    split_qt_hi(i + 1, 0)
                    copy_pt(i, 1, 0)
                    copy_pt(i, 1, 1)
                split_y_hi(i, 1)
                if nxt:
                    split_qt_hi(i + 1, 1)
                    copy_v(i + 1)

            slot(0, True, True)
            with act.Fori(1, B - 2) as i:
                slot(i, True, True)
            slot(B - 2, True, False)
            slot(B - 1, False, False)

        @block.vector
        def _(dve):
            def row_stats(b):
                dve.wait_ge(x_loaded, 16 * (b + 1))
                for n in range(2):
                    dve.bn_stats(stats[:, n, :], xs[:, n * N2:(n + 1) * N2]).then_inc(half_stats, 1)

            def mean_and_variance(b):
                dve.bn_aggr(mean_var[:, :], stats[:, :, :].rearrange("p a s -> p (a s)")
                            ).then_inc(mean_done, 1)
                dve.wait_ge(mean_done, b + 1)
                dve.tensor_scalar(var_eps[:, :], mean_var[:, 1:2], LN_EPS, None, ALU.add
                                  ).then_inc(var_ready, 1)

            def copy_ada(a):
                dve.wait_ge(ada_done, KC * (a + 1))
                dve.tensor_copy(ada_nat[:, a, :], Y_BANK[a][:, :]).then_inc(ada_copied, 1)

            def add_ada_bias(a):
                dve.wait_ge(ada_turned, a + 1)
                place = mod_all[:, :, a * KC:(a + 1) * KC].rearrange("p b (h j) -> p h j b", h=2)
                dve.tensor_tensor(place, Q_BANK[a][:, :].rearrange("p (j h b) -> p h j b", h=2, b=B),
                                  bias[:, a * KC:(a + 1) * KC].rearrange("p (h j o) -> p h j o", h=2, o=1)
                                  .broadcast_to([P, 2, 4, B]), ALU.add
                                  ).then_inc(mod_biased if a == 0 else mod_ready, 1)
                if a == 0:
                    dve.wait_ge(mod_biased, 1)
                    dve.tensor_scalar(mod_all[:, :, 0:KC], mod_all[:, :, 0:KC], 1.0, None, ALU.add
                                      ).then_inc(mod_ready, 1)

            def split_lo(chunk):
                dve.wait_ge(hi_split, SPLIT.index(chunk) + 1)
                dve.tensor_tensor(split_of(chunk)(1), ring[:, ring_slot(chunk), :], split_of(chunk)(0).bitcast(F32),
                                  ALU.subtract).then_inc(lo_split, 1)

            def modulate_upper(b, scale, shift):
                dve.wait_ge(xn_ready, b + 1)
                for k in range(4, 8):
                    h = dve.tensor_scalar(xt[:, k, :], xt[:, k, :],
                                          scale(k), shift(k), ALU.mult, ALU.add)
                h.then_inc(h_upper, 1)

            def split_h(b):
                if again(b):
                    dve.wait_ge(q_done, 2 * b)
                for half in range(2):
                    if half == 0:
                        dve.wait_ge(h_lower, b + 1)
                    else:
                        dve.wait_ge(h_upper, b + 1)
                    ks = slice(4 * half, 4 * half + 4)
                    dve.tensor_copy(ht[:, 0, ks, :], xt[:, ks, :]).then_inc(h_hi, 1)
                for half in range(2):
                    ks = slice(4 * half, 4 * half + 4)
                    dve.wait_ge(h_hi, 2 * b + half + 1)
                    dve.tensor_tensor(ht[:, 1, ks, :], xt[:, ks, :], ht[:, 0, ks, :].bitcast(F32),
                                      ALU.subtract).then_inc(ht_ready, 1)

            def copy_ckv(b):
                dve.wait_ge(ckv_done, b + 1)
                if again(b):
                    dve.wait_ge(q_ready, 2 * b)
                dve.tensor_copy(ckv, Cb[:, 0:LATENT]).then_inc(ckv_ready, 1)

            def split_ckvt(b):
                dve.wait_ge(ckvt_done, b + 1)
                src = D[:, 0:LATENT].rearrange("p (k t) -> p k t", t=P)
                dve.tensor_copy(ckvt[:, 0, :, :], src).then_inc(ckvt_hi, 1)
                dve.wait_ge(ckvt_hi, b + 1)
                dve.tensor_tensor(ckvt[:, 1, :, :], src, ckvt[:, 0, :, :].bitcast(F32), ALU.subtract
                                  ).then_inc(ckvt_ready, 1)

            def split_kt_lo(b):
                dve.wait_ge(kt_hi, b + 1)
                for side in range(2):
                    rows, cols = slice(side * HEAD, (side + 1) * HEAD), slice(side * P, (side + 1) * P)
                    lo = dve.tensor_tensor(kt[rows, 1, :, cols],
                                           D[rows, 0:2 * P].rearrange("d (p s) -> d p s", s=P),
                                           kt[rows, 0, :, cols].bitcast(F32), ALU.subtract)
                lo.then_inc(kt_ready, 1)

            def split_qt_lo(b, n):
                dve.wait_ge(qt_hi, 2 * b + n + 1)
                cs = slice(4 * n, 4 * n + 4)
                dve.tensor_tensor(qt[:, 1, cs, :], Q_BANK[n][:, :].rearrange("p (j t) -> p j t", t=P),
                                  qt[:, 0, cs, :].bitcast(F32), ALU.subtract).then_inc(qt_ready, 1)

            def heads(ap):
                return ap.rearrange("p (h d) -> p h d", d=HEAD)

            def turn(src, straight, factor, signal):
                n = heads(src).shape[1]
                dve.scalar_tensor_tensor(heads(straight), heads(src), factor,
                                         tables[:, 0:1, :].broadcast_to([P, n, HEAD]), ALU.mult, ALU.mult)
                for a in range(2):
                    mine, other = slice(a * HALF, (a + 1) * HALF), slice((1 - a) * HALF, (2 - a) * HALF)
                    last = dve.scalar_tensor_tensor(
                        heads(turned[:, 0:n * HEAD])[:, :, mine], heads(src)[:, :, other], factor,
                        tables[:, 1:2, mine].broadcast_to([P, n, HALF]), ALU.mult, ALU.mult)
                last.then_inc(signal, 1)

            def turn_q(b, n):
                dve.wait_ge(q_done, 2 * b + n + 1)
                turn(Q_BANK[n][:, :], q_nat[:, n * N2:(n + 1) * N2], 1.0, q_times_table)

            def turn_k(b):
                dve.wait_ge(kv_done, b + 1)
                turn(Cb[:, 0:LATENT], k_nat, HEAD ** -0.5, k_times_table)

            def maxima(b, e):
                dve.wait_ge(s_done, 4 * b + e + 1)
                if again(b):
                    dve.wait_ge(exp_done, 4 * (b - 1) + e + 1)
                dve.tensor_reduce(neg_max[:, 4 * e:4 * e + 4],
                                  s_bank(b, e // 2, e % 2)[:, :].rearrange("p (r s) -> p r s", s=P),
                                  AX.X, ALU.max, negate=True).then_inc(max_ready, 1)

            def invert(b, p):
                dve.wait_ge(exp_done, 4 * b + 2 * p + 2)
                if again(b):
                    dve.wait_ge(probs_ready, 4 * (b - 1) + 2 * p + 2)
                cols = slice(8 * p, 8 * p + 8)
                dve.reciprocal(inv_sums[:, cols], sums[:, cols]).then_inc(inv_ready, 1)

            def split_y_lo(b, p):
                dve.wait_ge(y_hi, 2 * b + p + 1)
                dve.tensor_tensor(yt[:, 1, p, :, :], Y_BANK[p][:, :].rearrange("p (j t) -> p j t", t=P),
                                  yt[:, 0, p, :, :].bitcast(F32), ALU.subtract).then_inc(y_ready, 1)

            def add_residual(b, n):
                dve.wait_ge(out_done, 2 * b + n + 1)
                if n == 0:
                    dve.wait_ge(res_loaded, 16 * (b + 1))
                cols = slice(n * N2, (n + 1) * N2)
                dve.tensor_tensor(res[:, cols], out_bank(b, n)[:, :], res[:, cols], ALU.add
                                  ).then_inc(out_added, 1)

            row_stats(0)
            dve.wait_ge(half_stats, 2)
            mean_and_variance(0)
            for chunk in SPLIT[:3 + EARLY_Q]:
                split_lo(chunk)
            dve.wait_ge(const_loaded, 48)
            copy_ada(0)
            add_ada_bias(0)
            copy_ada(1)
            add_ada_bias(1)
            dve.wait_ge(mod_ready, 2)
            modulate_upper(0, lambda k: mod_all[:, 0, k:k + 1], lambda k: mod_all[:, 0, KC + k:KC + k + 1])
            split_h(0)
            row_stats(1)
            dve.wait_ge(half_stats, 4)
            dve.wait_ge(stats_turned, 1)
            split_lo(("q", 4))
            mean_and_variance(1)
            split_lo(("q", 5))
            copy_ckv(0)
            split_lo(("q", 6))
            split_ckvt(0)
            split_lo(("q", 7))
            split_lo(("o", 0))
            row_stats(2)
            turn_k(0)
            dve.wait_ge(half_stats, 6)
            dve.wait_ge(stats_turned, 2)
            modulate_upper(1, lambda k: mod_all[:, 1, k:k + 1], lambda k: mod_all[:, 1, KC + k:KC + k + 1])
            mean_and_variance(2)
            split_lo(("o", 2))
            dve.wait_ge(kt_done, 1)
            turn_q(0, 0)
            dve.wait_ge(kt_zeroed, 1)
            split_kt_lo(0)
            split_h(1)
            split_qt_lo(0, 0)
            dve.wait_ge(q_ready, 1)
            turn_q(0, 1)
            split_lo(("o", 4))
            maxima(0, 0)
            maxima(0, 1)
            invert(0, 0)

            def slot(i, nxt, nxt2, nxt3):
                if nxt:
                    copy_ckv(i + 1)
                    if not again(i):
                        split_qt_lo(0, 1)
                        split_lo(("o", 5))
                    split_ckvt(i + 1)
                if not again(i):
                    split_lo(("o", 6))
                if nxt:
                    turn_q(i + 1, 0)
                if not again(i):
                    split_lo(("o", 7))
                if nxt:
                    maxima(i, 2)
                    maxima(i, 3)
                    dve.wait_ge(q_ready, 2 * i + 3)
                    turn_k(i + 1)
                if nxt2:
                    dve.wait_ge(mod_loaded, 16 * (i + 1))
                    modulate_upper(i + 2, lambda k: mod[:, k:k + 1], lambda k: mod[:, KC + k:KC + k + 1])
                if nxt:
                    invert(i, 1)
                split_y_lo(i, 0)
                if nxt:
                    dve.wait_ge(kt_done, i + 2)
                    turn_q(i + 1, 1)
                    split_kt_lo(i + 1)
                    split_qt_lo(i + 1, 0)
                split_y_lo(i, 1)
                if nxt:
                    split_qt_lo(i + 1, 1)
                if nxt2:
                    split_h(i + 2)
                if nxt:
                    maxima(i + 1, 0)
                    maxima(i + 1, 1)
                add_residual(i, 0)
                if nxt and last_row(i + 1):
                    maxima(i + 1, 2)
                    maxima(i + 1, 3)
                if nxt3:
                    row_stats(i + 3)
                    dve.wait_ge(half_stats, 2 * i + 8)
                    dve.wait_ge(stats_turned, i + 3)
                if nxt:
                    invert(i + 1, 0)
                    if last_row(i + 1):
                        invert(i + 1, 1)
                add_residual(i, 1)
                if nxt3:
                    mean_and_variance(i + 3)

            slot(0, True, True, True)
            with dve.Fori(1, B - 3) as i:
                slot(i, True, True, True)
            slot(B - 3, True, True, False)
            slot(B - 2, True, False, False)
            slot(B - 1, False, False, False)

        @block.gpsimd
        def _(pool):
            def inverse_deviation(b):
                pool.wait_ge(var_ready, b + 1)
                pool.tensor_tensor(rstd[:, :], var_eps[:, :], minus_half[:, :], ALU.pow
                                   ).then_inc(rstd_ready, 1)

            def normalise_x(b):
                pool.wait_ge(xt_loaded, 16 * (b + 1))
                pool.wait_ge(stats_ready, b + 1)
                pool.tensor_tensor(xt[:, :, :], xt[:, :, :], mean_rstd[:, 0:1, :].broadcast_to([P, KC, P]),
                                   ALU.subtract).then_inc(centred, 1)
                pool.wait_ge(centred, b + 1)
                pool.tensor_tensor(xt[:, :, :], xt[:, :, :], mean_rstd[:, 1:2, :].broadcast_to([P, KC, P]),
                                   ALU.mult).then_inc(xn_ready, 1)

            def normalise_probs(b, e):
                if e % 2 == 0:
                    pool.wait_ge(inv_ready, 2 * b + e // 2 + 1)
                tiles = probs_of(b, e // 2)[:, 2 * (e % 2):2 * (e % 2) + 2, :, :].rearrange("p j h s -> p (j h) s")
                pool.tensor_tensor(tiles, tiles, inv_sums[:, 4 * e:4 * e + 4].rearrange("p (r o) -> p r o", o=1)
                                   .broadcast_to([P, 4, P]), ALU.mult).then_inc(probs_ready, 1)

            def add_q(b, n):
                pool.wait_ge(q_times_table, 2 * b + n + 1)
                cols = slice(n * N2, (n + 1) * N2)
                pool.tensor_tensor(q_nat[:, cols], q_nat[:, cols], turned[:, :], ALU.add
                                   ).then_inc(q_ready, 1)

            def add_k(b):
                pool.wait_ge(k_times_table, b + 1)
                pool.tensor_tensor(k_nat, k_nat, turned[:, 0:LATENT], ALU.add).then_inc(k_ready, 1)

            def split_lo(chunk):
                pool.wait_ge(hi_split, SPLIT.index(chunk) + 1)
                pool.tensor_tensor(split_of(chunk)(1), ring[:, ring_slot(chunk), :], split_of(chunk)(0).bitcast(F32),
                                   ALU.subtract).then_inc(pool_split, 1)

            pool.memset(ident[:, :], 0.0).then_inc(ident_zero, 1)
            pool.wait_ge(ident_zero, 1)
            pool.affine_select(out=ident[:, :], in_=ident[:, :], compare_op=ALU.not_equal, fill=1.0,
                               base=0, pattern=[[-1, P]], channel_multiplier=1).then_inc(ident_ready, 1)
            pool.memset(minus_half[:, :], -0.5).then_inc(half_set, 1)
            pool.wait_ge(half_set, 1)
            inverse_deviation(0)
            normalise_x(0)
            pool.memset(kt[:, :, :, :].bitcast(F32), 0.0).then_inc(kt_zeroed, 1)
            split_lo(("q", 2))
            split_lo(("q", 3))
            inverse_deviation(1)
            normalise_x(1)
            split_lo(("o", 1))
            add_k(0)
            inverse_deviation(2)
            add_q(0, 0)
            split_lo(("o", 3))
            add_q(0, 1)

            def slot(i, nxt, nxt2, nxt3):
                normalise_probs(i, 0)
                normalise_probs(i, 1)
                if nxt2:
                    normalise_x(i + 2)
                if nxt:
                    add_q(i + 1, 0)
                    add_k(i + 1)
                normalise_probs(i, 2)
                normalise_probs(i, 3)
                if nxt:
                    add_q(i + 1, 1)
                if nxt3:
                    inverse_deviation(i + 3)

            slot(0, True, True, True)
            with pool.Fori(1, B - 3) as i:
                slot(i, True, True, True)
            slot(B - 3, True, True, False)
            slot(B - 2, True, False, False)
            slot(B - 1, False, False, False)


def rope_tables(tokens):
    import numpy as np

    freqs = (np.float32(1.0) / np.float32(10000.0) ** (np.arange(0, HEAD, 2, dtype=np.float32)
                                                       / np.float32(HEAD))).astype(np.float32)
    emb = np.arange(tokens, dtype=np.float32)[:, None] * freqs[None, :]
    cos, sin = np.cos(emb), np.sin(emb)
    return np.ascontiguousarray(np.stack([np.concatenate([cos, cos], axis=-1),
                                          np.concatenate([-sin, sin], axis=-1)], axis=1), dtype=np.float32)


def kernel(**inputs):
    import numpy as np
    import concourse.bacc as bacc
    from concourse.bass_utils import run_bass_kernel_spmd

    x = np.ascontiguousarray(inputs["x"])
    rows, tokens, width = x.shape
    tiles = width // P

    def by_pairs(w):
        return w.reshape(KV // 2, 2, PER_KV, HEAD, -1).transpose(0, 2, 1, 3, 4).reshape(width, -1)

    w_q = by_pairs(np.asarray(inputs["L0_cond_Wq"])).T
    w_o = by_pairs(np.asarray(inputs["L0_cond_Wo"]).T)
    w_kd = np.asarray(inputs["L0_cond_Wkd"]).T
    w_kv = np.concatenate([np.asarray(inputs["L0_cond_Wku"]).T, np.asarray(inputs["L0_cond_Wvu"]).T], axis=1)
    w_ada = np.asarray(inputs["L0_cond_W_ada"])
    per = width // LATENT
    arrays = {
        "in_x": x,
        "in_x_t": x.reshape(rows, tokens, tiles, P).transpose(0, 3, 2, 1),
        "in_cond_t": np.asarray(inputs["cond_2048"]).reshape(rows, tiles, P).transpose(2, 1, 0),
        "in_w_ada": w_ada.reshape(2, width, tiles, P).transpose(0, 2, 3, 1).reshape(2 * tiles, P, width),
        "in_b_ada": np.asarray(inputs["L0_cond_b_ada"]).reshape(2 * tiles, P).T,
        "in_w_q": w_q.reshape(tiles, P, width),
        "in_w_kd": w_kd.reshape(tiles // per, per, P, LATENT).transpose(0, 2, 1, 3).reshape(tiles // per, P, width),
        "in_w_kv": w_kv.reshape(LATENT // P, P, 2 * LATENT).transpose(1, 0, 2).reshape(P, width),
        "in_w_o": w_o.reshape(tiles, P, width),
        "in_rope": rope_tables(tokens),
    }
    arrays = {n: np.ascontiguousarray(a) for n, a in arrays.items()}
    nc = bacc.Bacc("TRN2", target_bir_lowering=False, num_devices=1)
    args = [nc.dram_tensor(n, a.shape, mybir.dt.from_np(a.dtype), kind="ExternalInput").ap()
            for n, a in arrays.items()]
    args.append(nc.dram_tensor("out_y", x.shape, F32, kind="ExternalOutput").ap())
    adaln_gqa_attention(nc, *args)
    return run_bass_kernel_spmd(nc, [arrays], core_ids=[0]).results[0]["out_y"]
```
